# Optimizing a Trainium2 kernel written in Bass

```python
import numpy as np
import jax
import jax.numpy as jnp

def _softmax(x, axis=-1):
    return jax.nn.softmax(x, axis=axis)

def _gelu(x):
    return jax.nn.gelu(x, approximate=True)

def _silu(x):
    return jax.nn.silu(x)

def _sigmoid(x):
    return jax.nn.sigmoid(x)

def _layernorm(x, axis=-1, eps=1e-05):
    m = jnp.mean(x, axis=axis, keepdims=True)
    v = jnp.var(x, axis=axis, keepdims=True)
    return (x - m) / jnp.sqrt(v + eps)

def _scatter_add(tgt, idx, src, axis=0):
    return tgt.at[idx].add(src)

def _segment_sum(src, seg, n):
    return jax.ops.segment_sum(src, seg, n)
kernel_name = 'mk_xattn_ffn_d1_seqx_r4_abb50d'

def setup_inputs(seed: int=0):
    np.random.seed(seed)
    _w = jnp.asarray

    def _rec_inputs():
        import jax
        import jax.numpy as jnp
        _rk = jax.random.key(seed)
        x = -0.0003929 + 0.9999 * jax.random.normal(jax.random.fold_in(_rk, 1), (16, 112, 256), jnp.float32)
        _lenS = 112 - jax.random.randint(jax.random.fold_in(_rk, 7), (16,), 0, max(1, 112 // 4) + 1, jnp.int32)
        _lenS2 = 375 - jax.random.randint(jax.random.fold_in(_rk, 8), (16,), 0, max(1, 375 // 4) + 1, jnp.int32)
        _ctx_512P = jax.random.normal(jax.random.fold_in(_rk, 11), (16, 16, 128), jnp.float32)
        _ctx_512c = jax.random.dirichlet(jax.random.fold_in(_rk, 511), 0.3 * jnp.ones((16,), jnp.float32), (16, 375))
        _ctx_512t = jnp.einsum('bsk,bkd->bsd', _ctx_512c, _ctx_512P)
        _ctx_512t = _ctx_512t * jax.lax.rsqrt(jnp.mean(jnp.square(_ctx_512t)) + 1e-12) * 0.953939
        ctx_512 = 4.13588e-05 + 0.999923 * (_ctx_512t + 0.3 * jax.random.normal(jax.random.fold_in(_rk, 611), (16, 375, 128), jnp.float32))
        return (x, ctx_512)
    x, ctx_512 = _rec_inputs()

    def _L0_xattn_setup():
        import jax, jax.numpy as jnp
        import numpy as np
        B, LQ, LK = (8, 512, 512)
        QD, KD, VD = (256, 128, 128)
        key = jax.random.key(seed)
        ks = jax.random.split(key, 9)
        s = 0.02
        return {'query': jax.random.normal(ks[0], (B, LQ, QD), jnp.float32), 'key': jax.random.normal(ks[1], (B, LK, KD), jnp.float32), 'value': jax.random.normal(ks[2], (B, LK, VD), jnp.float32), 'Wq': jax.random.normal(ks[3], (QD, QD), jnp.float32) * s, 'bq': jnp.zeros((QD,), jnp.float32), 'Wk': jax.random.normal(ks[4], (KD, QD), jnp.float32) * s, 'bk': jnp.zeros((QD,), jnp.float32), 'Wv': jax.random.normal(ks[5], (VD, QD), jnp.float32) * s, 'bv': jnp.zeros((QD,), jnp.float32)}
    _L0_xattn_all = _L0_xattn_setup()
    _L0_xattn_in = {k: v for k, v in _L0_xattn_all.items() if k in ('Wq', 'bq', 'Wk', 'bk', 'Wv', 'bv')}
    del _L0_xattn_all

    def _L0_ffn_setup():
        import jax, jax.numpy as jnp
        import numpy as np
        FP8_MAX = 448.0
        FP8 = jnp.float8_e4m3fn
        key = jax.random.key(seed)
        kx, kw, kb = jax.random.split(key, 3)
        B, S, D_in, D_out = (4, 2048, 256, 256)
        x = jax.random.normal(kx, (B, S, D_in), dtype=jnp.float32)
        w = jax.random.normal(kw, (D_out, D_in), dtype=jnp.float32) * 0.02
        weight_scale = jnp.maximum(jnp.max(jnp.abs(w)), 1e-12) / FP8_MAX
        weight = (w / weight_scale).astype(FP8)
        bias = jax.random.normal(kb, (D_out,), dtype=jnp.float32) * 0.01
        return {'x': x, 'weight': weight, 'weight_scale': weight_scale, 'bias': bias}
    _L0_ffn_all = _L0_ffn_setup()
    _L0_ffn_in = {k: v for k, v in _L0_ffn_all.items() if k in ('weight', 'weight_scale', 'bias')}
    del _L0_ffn_all
    return {'x': x, 'ctx_512': ctx_512, 'L0_xattn_Wq': _L0_xattn_in['Wq'], 'L0_xattn_bq': _L0_xattn_in['bq'], 'L0_xattn_Wk': _L0_xattn_in['Wk'], 'L0_xattn_bk': _L0_xattn_in['bk'], 'L0_xattn_Wv': _L0_xattn_in['Wv'], 'L0_xattn_bv': _L0_xattn_in['bv'], 'L0_ffn_weight': _L0_ffn_in['weight'], 'L0_ffn_weight_scale': _L0_ffn_in['weight_scale'], 'L0_ffn_bias': _L0_ffn_in['bias']}

def reference(x, ctx_512, L0_xattn_Wq, L0_xattn_bq, L0_xattn_Wk, L0_xattn_bk, L0_xattn_Wv, L0_xattn_bv, L0_ffn_weight, L0_ffn_weight_scale, L0_ffn_bias):
    import jax
    import jax.numpy as jnp

    def _L0_xattn_ref(query, key, value, Wq, bq, Wk, bk, Wv, bv):
        import jax, jax.numpy as jnp
        import numpy as np
        B, LQ, LK = (8, 512, 512)
        QD, KD, VD = (256, 128, 128)
        q = jnp.einsum('bld,de->ble', query, Wq) + bq
        k = jnp.einsum('bld,de->ble', key, Wk) + bk
        v = jnp.einsum('bld,de->ble', value, Wv) + bv
        scores = jnp.einsum('bqe,bke->bqk', q, k)
        attn = jax.nn.softmax(scores, axis=-1)
        out = jnp.einsum('bqk,bke->bqe', attn, v)
        return out

    def _L0_ffn_ref(x, weight, weight_scale, bias):
        import jax, jax.numpy as jnp
        import numpy as np
        FP8_MAX = 448.0
        FP8 = jnp.float8_e4m3fn
        amax = jnp.max(jnp.abs(x), axis=-1, keepdims=True)
        x_scale = jnp.maximum(amax, 1e-12) / FP8_MAX
        qinput = (x / x_scale).astype(FP8)
        A = qinput.astype(x.dtype) * x_scale
        Bm = weight.astype(x.dtype) * weight_scale
        out = jnp.einsum('bsk,nk->bsn', A, Bm) + bias
        return out.astype(x.dtype)
    x = x + _L0_xattn_ref(_layernorm(x, axis=-1), ctx_512, ctx_512, L0_xattn_Wq, L0_xattn_bq, L0_xattn_Wk, L0_xattn_bk, L0_xattn_Wv, L0_xattn_bv)
    x = x + _L0_ffn_ref(_layernorm(x, axis=-1), L0_ffn_weight, L0_ffn_weight_scale, L0_ffn_bias)
    return x

_drawn_inputs = setup_inputs


def setup_inputs(seed=0):
    import zlib

    import numpy as np

    out = dict(_drawn_inputs(seed))
    spreads = {'L0_xattn_bq': (0.0, 0.377), 'L0_xattn_bk': (0.0, 0.8), 'L0_xattn_bv': (0.0, 0.1)}
    factors = {'L0_ffn_bias': 5.937}
    for name, (base, spread) in spreads.items():
        noise = np.random.default_rng([zlib.crc32(name.encode()), seed]).standard_normal(out[name].shape)
        drawn = base * np.exp(spread * noise) if base else spread * noise
        out[name] = jnp.asarray(drawn.astype(out[name].dtype))
    for name, factor in factors.items():
        out[name] = (out[name] * factor).astype(out[name].dtype)
    return out
```

```python
import concourse.bass as bass
from concourse import mybir
from contextlib import ExitStack

B, Q, DX = 16, 112, 256
K, DC = 375, 128
KP, KJ = 125, 3
PAIRS = B // 2
XC = DX // 128
FP8_MAX = 448.0
EPS = 1e-5
AMAX_FLOOR = 1e-12


class Pair:

    def __init__(self, half, k):
        self.half, self.k = half + k // 2, k % 2

    def __add__(self, d):
        return Pair(self.half, self.k + d)

    @property
    def n(self):
        return 2 * self.half + self.k

    @property
    def known(self):
        return isinstance(self.half, int)

    def within(self):
        return not self.known or 0 <= self.n < PAIRS

    def batches(self, h):
        return 4 * self.half + 2 * self.k + h


def xattn_ffn_kernel(nc, x, ctx, ctx_t, wq_t, wk_t, wv, bq, bk, bv, w_t, w_scale, bias, out):
    fp32, bf16 = mybir.dt.float32, mybir.dt.bfloat16
    u8, u16, u32 = mybir.dt.uint8, mybir.dt.uint16, mybir.dt.uint32
    ALU, ACT, AX = mybir.AluOpType, mybir.ActivationFunctionType, mybir.AxisListType

    stack = ExitStack()
    with stack:
        def sb(name, shape, dt=fp32):
            return stack.enter_context(nc.sbuf_tensor(name, shape, dt))

        def ps(name, shape, dt=fp32):
            return stack.enter_context(nc.psum_tensor(name, shape, dt))

        def sem(name):
            return stack.enter_context(nc.semaphore(name))

        ident = sb("ident", [128, 128])
        ident_b = sb("ident_b", [128, 128], bf16)
        wq_ts = sb("wq_ts", [128, XC, DX])
        wk_ts = sb("wk_ts", [128, XC, DC])
        bq_s = sb("bq_s", [128, XC])
        wqk = sb("wqk", [128, XC, DC])
        bqk = sb("bqk", [128, 1])
        wv_s = sb("wv_s", [128, DX])
        bv_b = sb("bv_b", [Q, DX])
        bias_b = sb("bias_b", [Q, DX])
        ws_s = sb("ws_s", [Q, 1])
        ws448 = sb("ws448", [Q, 1])
        eps_s = sb("eps_s", [Q, 1])
        w8 = sb("w8", [128, XC, DX], u8)
        w_bits = sb("w_bits", [128, XC, DX], u32)
        w_mag = sb("w_mag", [128, XC, DX], u32)
        w_sub = sb("w_sub", [128, XC, DX])
        w_abs = sb("w_abs", [128, XC, DX])
        w_sign = sb("w_sign", [128, XC, DX], u32)
        w_b = sb("w_b", [128, XC, DX], bf16)

        x_s = [sb(f"x_s{i}", [Q, 2, DX]) for i in range(2)]
        ctx_s = [sb(f"ctx_s{i}", [KP, KJ, DC]) for i in range(4)]
        ctx_ts = [sb(f"ctx_ts{i}", [DC, K]) for i in range(4)]
        st1 = [sb(f"st1_{i}", [Q, 2, 6]) for i in range(2)]
        mv1 = [sb(f"mv1_{i}", [Q, 2, 2]) for i in range(2)]
        ln1 = [sb(f"ln1_{i}", [Q, 2]) for i in range(2)]
        rstd1 = [sb(f"rstd1_{i}", [Q, 2]) for i in range(2)]
        nmr1 = [sb(f"nmr1_{i}", [Q, 2]) for i in range(2)]
        xn = [sb(f"xn{i}", [Q, 2, DX]) for i in range(2)]
        xn_t = sb("xn_t", [128, XC, 2 * Q])
        tq_t = [sb(f"tq_t{i}", [DC, 2, Q]) for i in range(2)]
        neg_max = sb("neg_max", [Q, 4])
        p_s = [sb(f"p_s{i}", [Q, K]) for i in range(2)]
        row_sum = sb("row_sum", [Q, 4])
        row_inv = sb("row_inv", [Q, 4])
        p_t = [sb(f"p_t{i}", [KP, KJ, Q]) for i in range(2)]
        u_t = [sb(f"u_t{i}", [DC, Q]) for i in range(2)]
        xb = [sb(f"xb{i}", [Q, 2, DX]) for i in range(2)]
        x1 = [sb(f"x1_{i}", [Q, 2, DX]) for i in range(2)]
        x1b = [sb(f"x1b_{i}", [Q, 2, DX]) for i in range(2)]
        sum2 = [sb(f"sum2_{i}", [Q, 2]) for i in range(2)]
        nmean2 = [sb(f"nmean2_{i}", [Q, 2]) for i in range(2)]
        xc = sb("xc", [Q, 2, DX])
        sq = sb("sq", [Q, DX])
        ssq = sb("ssq", [Q, 2])
        ln2 = sb("ln2", [Q, 2])
        rstd2 = sb("rstd2", [Q, 2])
        amax = sb("amax", [Q, 2])
        hmax = sb("hmax", [Q, 2])
        hmax1 = sb("hmax1", [Q, 2])
        hinv = sb("hinv", [Q, 2])
        qscale = sb("qscale", [Q, 2])
        qscale20 = sb("qscale20", [Q, 2])
        oscale = [sb(f"oscale{i}", [Q, 2]) for i in range(2)]
        mag = sb("mag", [Q, 2, DX], bf16)
        power = sb("power", [Q, 2, DX], bf16)
        magic = sb("magic", [Q, 2, DX], bf16)
        shifted = sb("shifted", [Q, 2, DX])
        quant = sb("quant", [Q, 2, DX], bf16)
        quant_t = sb("quant_t", [128, XC, 2, Q], bf16)
        o_s = [sb(f"o_s{i}", [Q, 2, DX]) for i in range(2)]

        ps_x = ps("ps_x", [128, 512])
        ps_s = [ps(f"ps_s{i}", [128, 512]) for i in range(2)]
        ps_p = ps("ps_p", [128, 512])
        ps_o = [ps(f"ps_o{i}", [128, 512]) for i in range(2)]
        ps_q = ps("ps_q", [128, 1024], bf16)
        ps_f = ps("ps_f", [128, 512])

        wqk_in, wv_in, rows_in, w8_in = sem("wqk_in"), sem("wv_in"), sem("rows_in"), sem("w8_in")
        x_in = [sem(f"x_in{i}") for i in range(2)]
        ctx_in = [sem(f"ctx_in{i}") for i in range(4)]
        ctx_t_in = [sem(f"ctx_t_in{i}") for i in range(4)]
        out_done = [sem(f"out_done{i}") for i in range(2)]
        ident_set, ident_ready = sem("ident_set"), sem("ident_ready")
        wqk_made, wqk_ready = sem("wqk_made"), sem("wqk_ready")
        ws_ready, w_step = sem("ws_ready"), sem("w_step")
        stats1, moments1, ln1_done, rstd1_ready = sem("stats1"), sem("moments1"), sem("ln1_done"), sem("rstd1_ready")
        nmr1_ready, xn_ready, xt_made, xt_ready = sem("nmr1_ready"), sem("xn_ready"), sem("xt_made"), sem("xt_ready")
        tq_made, tq_ready = sem("tq_made"), sem("tq_ready")
        scores_made, max_ready, probs_ready = sem("scores_made"), sem("max_ready"), sem("probs_ready")
        inv_ready, pt_made, pt_ready = sem("inv_ready"), sem("pt_made"), sem("pt_ready")
        ut_made, ut_ready, attn_made = sem("ut_made"), sem("ut_ready"), sem("attn_made")
        xb_ready, x1_ready, x1b_ready = sem("xb_ready"), sem("x1_ready"), sem("x1b_ready")
        nmean2_ready, xc_ready, ssq_ready, ln2_done = sem("nmean2_ready"), sem("xc_ready"), sem("ssq_ready"), sem("ln2_done")
        rstd2_ready, amax_ready, scale_step = sem("rstd2_ready"), sem("amax_ready"), sem("scale_step")
        mag_ready, magic_ready, shifted_ready = sem("mag_ready"), sem("magic_ready"), sem("shifted_ready")
        quant_ready, qt_made, qt_ready = sem("quant_ready"), sem("qt_made"), sem("qt_ready")
        ffn_made, out_ready = sem("ffn_made"), sem("out_ready")
        SCALE_STEPS = 6

        ctx_rows = ctx.rearrange("b (p j) d -> b p j d", j=KJ)
        x_rows = x.rearrange("(n h) q d -> n q h d", h=2)
        out_rows = out.rearrange("(n h) q d -> n q h d", h=2)
        KP0 = 112

        def pipeline(engine, steps):
            for u in (-1, 0, 1):
                steps(Pair(0, u))
            with engine.Fori(1, PAIRS // 2 - 1) as half:
                steps(Pair(half, 0))
                steps(Pair(half, 1))
            for u in range(PAIRS - 2, PAIRS + 2):
                steps(Pair(0, u))

        block = stack.enter_context(nc.Block())

        @block.sync
        def _(sp):
            def load_x(p):
                if not p.known or p.n >= 2:
                    sp.wait_ge(xn_ready, 2 * (p.n - 1))
                    sp.wait_ge(xb_ready, p.n - 1)
                sp.dma_start(x_s[p.k][:], x_rows[p.n]).then_inc(x_in[p.k], 16)

            def load_ctx_t(p, h):
                slot = 2 * p.k + h
                if not p.known or p.n >= 2:
                    sp.wait_ge(scores_made, p.batches(h) - 3)
                sp.dma_start(ctx_ts[slot][:], ctx_t[p.batches(h)]).then_inc(ctx_t_in[slot], 16)

            def load_ctx(p, h):
                slot = 2 * p.k + h
                if not p.known or p.n >= 2:
                    sp.wait_ge(ut_made, p.batches(h) - 3)
                sp.dma_start(ctx_s[slot][0:KP0], ctx_rows[p.batches(h), 0:KP0]).then_inc(ctx_in[slot], 16)
                sp.dma_start(ctx_s[slot][KP0:KP], ctx_rows[p.batches(h), KP0:KP]).then_inc(ctx_in[slot], 16)

            def store(p):
                sp.wait_ge(out_ready, 2 * (p.n + 1))
                sp.dma_start(out_rows[p.n], o_s[p.k][:]).then_inc(out_done[p.k], 16)

            def step(p):
                load_x(p)
                for h in range(2):
                    load_ctx_t(p, h)
                    load_ctx(p, h)
                if not p.known or p.n >= 4:
                    store(p + -4)

            load_x(Pair(0, 0))
            sp.dma_start(wq_ts[:], wq_t.rearrange("(c p) n -> p c n", p=128)).then_inc(wqk_in, 16)
            sp.dma_start(wk_ts[:], wk_t.rearrange("(c p) n -> p c n", p=128)).then_inc(wqk_in, 16)
            sp.dma_start(bq_s[:], bq).then_inc(wqk_in, 16)
            load_ctx_t(Pair(0, 0), 0)
            load_ctx(Pair(0, 0), 0)
            sp.dma_start(bv_b[:], bv.rearrange("(a n) -> a n", a=1).broadcast_to([Q, DX])).then_inc(rows_in, 16)
            sp.dma_start(wv_s[:], wv).then_inc(wv_in, 16)
            load_ctx_t(Pair(0, 0), 1)
            load_ctx(Pair(0, 0), 1)
            load_x(Pair(0, 1))
            sp.dma_start(w8[:], w_t.rearrange("(c p) n -> p c n", p=128)).then_inc(w8_in, 16)
            sp.dma_start(bias_b[:], bias.rearrange("(a n) -> a n", a=1).broadcast_to([Q, DX])).then_inc(rows_in, 16)
            sp.dma_start(ws_s[:], w_scale.broadcast_to([Q, 1])).then_inc(rows_in, 16)
            for h in range(2):
                load_ctx_t(Pair(0, 1), h)
                load_ctx(Pair(0, 1), h)
            for n in (2, 3):
                step(Pair(0, n))
            with sp.Fori(2, PAIRS // 2) as half:
                step(Pair(half, 0))
                step(Pair(half, 1))
            for n in range(PAIRS - 4, PAIRS):
                store(Pair(0, n))
            for i in range(2):
                sp.wait_ge(out_done[i], 16 * PAIRS // 2)

        @block.gpsimd
        def _(pool):
            for m in (ident, ident_b):
                pool.memset(m[:], 0.0).then_inc(ident_set, 1)
            for n, m in enumerate((ident, ident_b)):
                pool.wait_ge(ident_set, n + 1)
                pool.affine_select(out=m[:], in_=m[:], compare_op=ALU.not_equal, fill=1.0, base=0,
                                   pattern=[[-1, 128]], channel_multiplier=1).then_inc(ident_ready, 1)

            def add_bv(p):
                pool.wait_ge(x_in[p.k], 16 * (p.half + 1))
                if not p.known or p.n >= 2:
                    pool.wait_ge(x1_ready, 2 * (p.n - 1))
                pool.tensor_tensor(xb[p.k][:], x_s[p.k][:], bv_b[:].unsqueeze(1).broadcast_to([Q, 2, DX]),
                                   ALU.add).then_inc(xb_ready, 1)

            def add_bias(p):
                pool.wait_ge(x1_ready, 2 * (p.n + 1))
                if not p.known or p.n >= 2:
                    pool.wait_ge(out_ready, 2 * (p.n - 1))
                pool.tensor_tensor(x1b[p.k][:], x1[p.k][:], bias_b[:].unsqueeze(1).broadcast_to([Q, 2, DX]),
                                   ALU.add).then_inc(x1b_ready, 1)

            def unshift(p):
                pool.wait_ge(shifted_ready, 2 * (p.n + 1))
                if not p.known or p.n >= 1:
                    pool.wait_ge(qt_made, p.n)
                pool.tensor_tensor(quant[:], shifted[:], magic[:], ALU.subtract).then_inc(quant_ready, 1)

            def steps(u):
                if u.within():
                    add_bv(u)
                if (u + -1).within():
                    add_bias(u + -1)
                    unshift(u + -1)

            pool.wait_ge(rows_in, 48)
            pipeline(pool, steps)

        @block.scalar
        def _(act):
            def rstd_1(p):
                act.wait_ge(moments1, 2 * (p.n + 1))
                act.activation(ln1[p.k][:], mv1[p.k][:, :, 1], ACT.Ln, bias=eps_s[:, 0:1]).then_inc(ln1_done, 1)
                act.wait_ge(ln1_done, p.n + 1)
                act.activation(rstd1[p.k][:], ln1[p.k][:], ACT.Exp, scale=-0.5).then_inc(rstd1_ready, 1)

            def norm_1(p):
                act.wait_ge(nmr1_ready, p.n + 1)
                if not p.known or p.n >= 2:
                    act.wait_ge(xt_made, p.n - 1)
                for h in range(2):
                    act.activation(xn[p.k][:, h], x_s[p.k][:, h], ACT.Identity, bias=nmr1[p.k][:, h:h + 1],
                                   scale=rstd1[p.k][:, h:h + 1]).then_inc(xn_ready, 1)

            def evict_xt(p):
                act.wait_ge(xt_made, p.n + 1)
                if not p.known or p.n >= 1:
                    act.wait_ge(tq_made, p.n)
                act.activation(xn_t[:], ps_x[:, 0:XC * 2 * Q], ACT.Copy).then_inc(xt_ready, 1)

            def evict_tq(p):
                act.wait_ge(tq_made, p.n + 1)
                if not p.known or p.n >= 2:
                    act.wait_ge(scores_made, 2 * (p.n - 1))
                act.activation(tq_t[p.k][:], ps_x[:, 0:2 * Q], ACT.Identity, bias=bqk[:, 0:1]).then_inc(tq_ready, 1)

            def exp(p, h):
                slot = 2 * p.k + h
                act.wait_ge(max_ready, p.batches(h) + 1)
                if not p.known or p.n >= 1:
                    act.wait_ge(pt_made, p.batches(h) - 1)
                act.activation(p_s[h][:], ps_s[h][0:Q, 0:K], ACT.Exp, bias=neg_max[:, slot:slot + 1],
                               accum_out=row_sum[:, slot:slot + 1]).then_inc(probs_ready, 1)

            def evict_pt(p, h):
                act.wait_ge(pt_made, p.batches(h) + 1)
                if not p.known or p.n >= 1:
                    act.wait_ge(ut_made, p.batches(h) - 1)
                act.activation(p_t[h][:], ps_p[0:KP, 0:KJ * Q], ACT.Copy).then_inc(pt_ready, 1)

            def evict_ut(p, h):
                act.wait_ge(ut_made, p.batches(h) + 1)
                if not p.known or p.n >= 1:
                    act.wait_ge(attn_made, p.batches(h) - 1)
                act.activation(u_t[h][:], ps_o[h][:, 0:Q], ACT.Copy).then_inc(ut_ready, 1)

            def center_2(p):
                act.wait_ge(nmean2_ready, p.n + 1)
                if not p.known or p.n >= 1:
                    act.wait_ge(shifted_ready, 2 * p.n)
                for h in range(2):
                    act.activation(xc[:, h], x1[p.k][:, h], ACT.Identity,
                                   bias=nmean2[p.k][:, h:h + 1]).then_inc(xc_ready, 1)
                for h in range(2):
                    act.wait_ge(xc_ready, 2 * p.n + h + 1)
                    if h or not p.known or p.n >= 1:
                        act.wait_ge(ssq_ready, 2 * p.n + h)
                    act.activation(sq[:], xc[:, h], ACT.Square, accum_out=ssq[:, h:h + 1]).then_inc(ssq_ready, 1)

            def rstd_2(p):
                act.wait_ge(ssq_ready, 2 * (p.n + 1))
                act.activation(ln2[:], ssq[:], ACT.Ln, bias=eps_s[:, 0:1], scale=1.0 / DX).then_inc(ln2_done, 1)
                act.wait_ge(ln2_done, p.n + 1)
                act.activation(rstd2[:], ln2[:], ACT.Exp, scale=-0.5).then_inc(rstd2_ready, 1)

            def evict_qt(p):
                act.wait_ge(qt_made, p.n + 1)
                if not p.known or p.n >= 1:
                    act.wait_ge(ffn_made, p.n)
                act.activation(quant_t[:], ps_q[:, 0:XC * 2 * Q], ACT.Copy).then_inc(qt_ready, 1)

            def steps(u):
                if (u + -1).within():
                    evict_pt(u + -1, 1)
                if u.within():
                    exp(u, 0)
                if (u + -1).within():
                    evict_ut(u + -1, 1)
                if (u + 1).within():
                    rstd_1(u + 1)
                if (u + -2).within():
                    evict_qt(u + -2)
                if (u + 1).within():
                    norm_1(u + 1)
                if (u + -1).within():
                    center_2(u + -1)
                if u.within():
                    exp(u, 1)
                if (u + -1).within():
                    rstd_2(u + -1)
                if (u + 1).within():
                    evict_xt(u + 1)
                if u.within():
                    evict_pt(u, 0)
                    evict_ut(u, 0)
                if (u + 1).within():
                    evict_tq(u + 1)

            act.wait_ge(wqk_made, 1)
            act.activation(wqk[:], ps_s[0][:, 0:XC * DC], ACT.Copy)
            act.activation(bqk[:], ps_s[0][:, XC * DC:XC * DC + 1], ACT.Copy).then_inc(wqk_ready, 1)
            act.wait_ge(wqk_ready, 1)
            act.wait_ge(ws_ready, 1)
            pipeline(act, steps)

        @block.vector
        def _(dve):
            def stats_1(p):
                dve.wait_ge(x_in[p.k], 16 * (p.half + 1))
                for h in range(2):
                    dve.bn_stats(st1[p.k][:, h], x_s[p.k][:, h]).then_inc(stats1, 1)

            def before_moments_1(p):
                dve.wait_ge(stats1, 2 * (p.n + 1))
                if not p.known or p.n >= 2:
                    dve.wait_ge(rstd1_ready, p.n - 1)

            def moments_1(p):
                for h in range(2):
                    dve.bn_aggr(mv1[p.k][:, h], st1[p.k][:, h]).then_inc(moments1, 1)

            def neg_mean_rstd_1(p):
                dve.wait_ge(rstd1_ready, p.n + 1)
                dve.wait_ge(moments1, 2 * (p.n + 1))
                if not p.known or p.n >= 2:
                    dve.wait_ge(xn_ready, 2 * (p.n - 1))
                dve.scalar_tensor_tensor(nmr1[p.k][:], mv1[p.k][:, :, 0], -1.0, rstd1[p.k][:],
                                         ALU.mult, ALU.mult).then_inc(nmr1_ready, 1)

            def row_max(p, h):
                slot = 2 * p.k + h
                dve.wait_ge(scores_made, p.batches(h) + 1)
                dve.tensor_reduce(neg_max[:, slot:slot + 1], ps_s[h][0:Q, 0:K], AX.X, ALU.max,
                                  negate=True).then_inc(max_ready, 1)

            def inverse_sum(p, h):
                slot = 2 * p.k + h
                dve.wait_ge(probs_ready, p.batches(h) + 1)
                dve.reciprocal(row_inv[:, slot:slot + 1], row_sum[:, slot:slot + 1]).then_inc(inv_ready, 1)

            def residual_1(p, h):
                slot = 2 * p.k + h
                dve.wait_ge(attn_made, p.batches(h) + 1)
                dve.wait_ge(inv_ready, p.batches(h) + 1)
                dve.wait_ge(xb_ready, p.n + 1)
                if not p.known or p.n >= 2:
                    dve.wait_ge(xc_ready, 2 * (p.n - 1))
                    dve.wait_ge(x1b_ready, p.n - 1)
                dve.scalar_tensor_tensor(x1[p.k][:, h], ps_o[h][0:Q, DC:DC + DX], row_inv[:, slot:slot + 1],
                                         xb[p.k][:, h], ALU.mult, ALU.add,
                                         accum_out=sum2[p.k][:, h:h + 1]).then_inc(x1_ready, 1)

            def neg_mean_2(p):
                dve.wait_ge(x1_ready, 2 * (p.n + 1))
                dve.tensor_scalar(nmean2[p.k][:], sum2[p.k][:], -1.0 / DX, None, ALU.mult).then_inc(nmean2_ready, 1)

            def abs_max(p):
                dve.wait_ge(xc_ready, 2 * (p.n + 1))
                dve.tensor_reduce(amax[:], xc[:], AX.X, ALU.max, apply_absolute_value=True).then_inc(amax_ready, 1)

            def scales(p):
                def after(i):
                    dve.wait_ge(scale_step, SCALE_STEPS * p.n + i)

                dve.wait_ge(amax_ready, p.n + 1)
                dve.wait_ge(rstd2_ready, p.n + 1)
                dve.tensor_tensor(hmax[:], amax[:], rstd2[:], ALU.mult).then_inc(scale_step, 1)
                after(1)
                dve.tensor_scalar(hmax1[:], hmax[:], AMAX_FLOOR, None, ALU.max).then_inc(scale_step, 1)
                after(2)
                dve.reciprocal(hinv[:], hmax1[:]).then_inc(scale_step, 1)
                if not p.known or p.n >= 2:
                    dve.wait_ge(out_ready, 2 * (p.n - 1))
                dve.tensor_scalar(oscale[p.k][:], hmax1[:], ws448[:, 0:1], None, ALU.mult).then_inc(scale_step, 1)
                after(3)
                dve.scalar_tensor_tensor(qscale[:], hinv[:], FP8_MAX, rstd2[:], ALU.mult, ALU.mult).then_inc(scale_step, 1)
                dve.scalar_tensor_tensor(qscale20[:], hinv[:], FP8_MAX * 2.0 ** 20, rstd2[:],
                                         ALU.mult, ALU.mult).then_inc(scale_step, 1)

            def quantise(p):
                dve.wait_ge(scale_step, SCALE_STEPS * (p.n + 1))
                for h in range(2):
                    dve.tensor_scalar(mag[:, h], xc[:, h], qscale20[:, h:h + 1], None, ALU.mult).then_inc(mag_ready, 1)
                dve.wait_ge(mag_ready, 2 * (p.n + 1))
                if not p.known or p.n >= 1:
                    dve.wait_ge(quant_ready, p.n)
                dve.tensor_scalar(power[:].bitcast(u16), mag[:].bitcast(u16), 0x7F80, 0x0040,
                                  ALU.bitwise_and, ALU.bitwise_or).then_inc(magic_ready, 1)
                dve.wait_ge(magic_ready, 2 * p.n + 1)
                dve.tensor_scalar(magic[:], power[:], 1.5 * 2.0 ** (20 - 6), None, ALU.max).then_inc(magic_ready, 1)
                dve.wait_ge(magic_ready, 2 * (p.n + 1))
                for h in range(2):
                    dve.scalar_tensor_tensor(shifted[:, h], xc[:, h], qscale[:, h:h + 1], magic[:, h],
                                             ALU.mult, ALU.add).then_inc(shifted_ready, 1)

            def residual_2(p, h):
                dve.wait_ge(ffn_made, p.n + 1)
                dve.wait_ge(x1b_ready, p.n + 1)
                if not p.known or p.n >= 2:
                    dve.wait_ge(out_done[p.k], 16 * p.half)
                dve.scalar_tensor_tensor(o_s[p.k][:, h], ps_f[0:Q, h * DX:(h + 1) * DX], oscale[p.k][:, h:h + 1],
                                         x1b[p.k][:, h], ALU.mult, ALU.add).then_inc(out_ready, 1)

            def decode_weights():
                def after(i):
                    dve.wait_ge(w_step, i)

                dve.wait_ge(w8_in, 16)
                dve.tensor_copy(w_bits[:], w8[:]).then_inc(w_step, 1)
                after(1)
                dve.tensor_scalar(w_mag[:], w_bits[:], 0x7F, 20, ALU.bitwise_and, ALU.logical_shift_left).then_inc(w_step, 1)
                dve.tensor_scalar(w_sign[:], w_bits[:], 0x80, 24, ALU.bitwise_and, ALU.logical_shift_left).then_inc(w_step, 1)
                after(2)
                dve.tensor_scalar(w_sub[:], w_mag[:], 7.0 * 2 ** 20, 2.0 ** -29, ALU.min, ALU.mult).then_inc(w_step, 1)
                after(4)
                dve.scalar_tensor_tensor(w_abs[:], w_mag[:].bitcast(fp32), 2.0 ** 120, w_sub[:],
                                         ALU.mult, ALU.max).then_inc(w_step, 1)
                after(5)
                dve.tensor_tensor(w_bits[:], w_abs[:].bitcast(u32), w_sign[:], ALU.bitwise_or).then_inc(w_step, 1)
                after(6)
                dve.tensor_copy(w_b[:], w_bits[:].bitcast(fp32)).then_inc(w_step, 1)

            def steps(u):
                if u.within():
                    row_max(u, 0)
                if (u + 1).within():
                    stats_1(u + 1)
                    before_moments_1(u + 1)
                if (u + -1).within():
                    inverse_sum(u + -1, 1)
                if (u + 1).within():
                    moments_1(u + 1)
                if (u + -1).within():
                    residual_1(u + -1, 1)
                    neg_mean_2(u + -1)
                if (u + 1).within():
                    neg_mean_rstd_1(u + 1)
                if u.known and u.n == -1:
                    decode_weights()
                    dve.wait_ge(rows_in, 48)
                    dve.tensor_scalar(ws448[:], ws_s[:], 1.0 / FP8_MAX, None, ALU.mult).then_inc(w_step, 1)
                    dve.wait_ge(w_step, 8)
                if u.within():
                    row_max(u, 1)
                if (u + -1).within():
                    abs_max(u + -1)
                if (u + -2).within():
                    residual_2(u + -2, 0)
                if (u + -1).within():
                    scales(u + -1)
                if (u + -2).within():
                    residual_2(u + -2, 1)
                if (u + -1).within():
                    quantise(u + -1)
                if u.within():
                    inverse_sum(u, 0)
                    residual_1(u, 0)

            dve.memset(eps_s[:], EPS).then_inc(ws_ready, 1)
            pipeline(dve, steps)

        @block.tensor
        def _(pe):
            def x_transpose(p):
                pe.wait_ge(xn_ready, 2 * (p.n + 1))
                if not p.known or p.n >= 1:
                    pe.wait_ge(tq_ready, p.n)
                for c in range(XC):
                    for h in range(2):
                        at = (2 * c + h) * Q
                        last = pe.transpose(ps_x[:, at:at + Q], xn[p.k][:, h, 128 * c:128 * (c + 1)], ident[0:Q, 0:Q])
                last.then_inc(xt_made, 1)

            def project(p):
                pe.wait_ge(xt_ready, p.n + 1)
                for c in range(XC):
                    last = pe.matmul(ps_x[:, 0:2 * Q], wqk[:, c], xn_t[:, c], start=c == 0, stop=c == XC - 1)
                last.then_inc(tq_made, 1)

            def scores(p, h):
                slot = 2 * p.k + h
                pe.wait_ge(tq_ready, p.n + 1)
                pe.wait_ge(ctx_t_in[slot], 16 * (p.half + 1))
                if not p.known or p.n >= 1:
                    pe.wait_ge(probs_ready, p.batches(h) - 1)
                pe.matmul(ps_s[h][0:Q, 0:K], tq_t[p.k][:, h], ctx_ts[slot][:], start=True, stop=True)\
                    .then_inc(scores_made, 1)

            def p_transpose(p, h):
                pe.wait_ge(probs_ready, p.batches(h) + 1)
                if h or not p.known or p.n >= 1:
                    pe.wait_ge(pt_ready, p.batches(h))
                for j in range(KJ):
                    last = pe.transpose(ps_p[0:KP, j * Q:(j + 1) * Q], p_s[h][:, j * KP:(j + 1) * KP], ident[0:Q, 0:Q])
                last.then_inc(pt_made, 1)

            def attend(p, h):
                slot = 2 * p.k + h
                pe.wait_ge(pt_ready, p.batches(h) + 1)
                pe.wait_ge(ctx_in[slot], 32 * (p.half + 1))
                if not p.known or p.n >= 1:
                    pe.wait_ge(x1_ready, p.batches(h) - 1)
                for j in range(KJ):
                    last = pe.matmul(ps_o[h][:, 0:Q], ctx_s[slot][:, j], p_t[h][:, j], start=j == 0, stop=j == KJ - 1)
                last.then_inc(ut_made, 1)

            def values(p, h):
                pe.wait_ge(ut_ready, p.batches(h) + 1)
                pe.matmul(ps_o[h][0:Q, DC:DC + DX], u_t[h][:], wv_s[:], start=True, stop=True).then_inc(attn_made, 1)

            def quant_transpose(p):
                pe.wait_ge(quant_ready, p.n + 1)
                if not p.known or p.n >= 1:
                    pe.wait_ge(qt_ready, p.n)
                for c in range(XC):
                    for h in range(2):
                        at = (2 * c + h) * Q
                        last = pe.transpose(ps_q[:, at:at + Q], quant[:, h, 128 * c:128 * (c + 1)], ident_b[0:Q, 0:Q])
                last.then_inc(qt_made, 1)

            def linear(p):
                pe.wait_ge(qt_ready, p.n + 1)
                if not p.known or p.n >= 1:
                    pe.wait_ge(out_ready, 2 * p.n)
                for h in range(2):
                    for c in range(XC):
                        last = pe.matmul(ps_f[0:Q, h * DX:(h + 1) * DX], quant_t[:, c, h], w_b[:, c],
                                         start=c == 0, stop=c == XC - 1)
                last.then_inc(ffn_made, 1)

            def steps(u):
                if u.within():
                    scores(u, 0)
                if (u + -1).within():
                    p_transpose(u + -1, 1)
                    attend(u + -1, 1)
                if (u + -2).within():
                    quant_transpose(u + -2)
                if (u + -1).within():
                    values(u + -1, 1)
                if u.within():
                    scores(u, 1)
                if (u + -2).within():
                    linear(u + -2)
                if (u + 1).within():
                    x_transpose(u + 1)
                if u.within():
                    p_transpose(u, 0)
                    attend(u, 0)
                if (u + 1).within():
                    project(u + 1)
                if u.within():
                    values(u, 0)

            pe.wait_ge(wqk_in, 48)
            for i in range(XC):
                for e in range(XC):
                    pe.matmul(ps_s[0][:, i * DC:(i + 1) * DC], wq_ts[:, e, 128 * i:128 * (i + 1)], wk_ts[:, e],
                              start=e == 0, stop=e == XC - 1)
            for e in range(XC):
                last = pe.matmul(ps_s[0][:, XC * DC:XC * DC + 1], wk_ts[:, e], bq_s[:, e:e + 1],
                                 start=e == 0, stop=e == XC - 1)
            last.then_inc(wqk_made, 1)
            pe.wait_ge(wqk_ready, 1)
            pe.wait_ge(ident_ready, 2)
            pe.wait_ge(wv_in, 16)
            pe.wait_ge(w_step, 7)
            pipeline(pe, steps)


def kernel(x, ctx_512, L0_xattn_Wq, L0_xattn_bq, L0_xattn_Wk, L0_xattn_bk, L0_xattn_Wv, L0_xattn_bv,
           L0_ffn_weight, L0_ffn_weight_scale, L0_ffn_bias):
    import numpy as np
    import concourse.bacc as bacc
    from concourse.bass_utils import run_bass_kernel_spmd

    ctx = np.asarray(ctx_512)
    arrays = {
        "x": np.asarray(x),
        "ctx": ctx,
        "ctx_t": ctx.reshape(B, KP, KJ, DC).transpose(0, 3, 2, 1).reshape(B, DC, K),
        "wq_t": np.asarray(L0_xattn_Wq).T,
        "wk_t": np.asarray(L0_xattn_Wk).T,
        "wv": np.asarray(L0_xattn_Wv),
        "bq": np.asarray(L0_xattn_bq).reshape(XC, 128).T,
        "bk": np.asarray(L0_xattn_bk),
        "bv": np.asarray(L0_xattn_bv),
        "w_t": np.asarray(L0_ffn_weight).T.view(np.uint8),
        "w_scale": np.asarray(L0_ffn_weight_scale).reshape(1, 1),
        "bias": np.asarray(L0_ffn_bias),
    }
    arrays = {f"in_{k}": np.ascontiguousarray(v) for k, v in arrays.items()}
    nc = bacc.Bacc("TRN2", target_bir_lowering=False, num_devices=1)
    args = [nc.dram_tensor(k, v.shape, mybir.dt.from_np(v.dtype), kind="ExternalInput").ap() for k, v in arrays.items()]
    args.append(nc.dram_tensor("out_0", (B, Q, DX), mybir.dt.float32, kind="ExternalOutput").ap())
    xattn_ffn_kernel(nc, *args)
    return run_bass_kernel_spmd(nc, [arrays], core_ids=[0]).results[0]["out_0"]
```

```python
import concourse.bass as bass
from concourse import mybir
from contextlib import ExitStack

B, Q, DX = 16, 112, 256
K, DC = 375, 128
KP, KJ = 125, 3
PAIRS = B // 2
XC = DX // 128
FP8_MAX = 448.0
EPS = 1e-5
AMAX_FLOOR = 1e-12


PAST = 2


class Pair:

    def __init__(self, half, k):
        self.half, self.k = half, k

    def back(self, pairs):
        return Pair(self.half, self.k - pairs)

    @property
    def n(self):
        return 2 * self.half + self.k

    @property
    def side(self):
        return self.k % 2

    @property
    def turn(self):
        return self.half + self.k // 2

    def exists(self):
        return not isinstance(self.half, int) or 0 <= self.n < PAIRS


def count(p, per=1, h=None, before=0):
    return 2 * per * p.half + (per * (p.k + PAST) + (per if h is None else h + 1) - before)


def xattn_ffn_kernel(nc, x, ctx, ctx_t, wq_t, wk_t, wv, bq, bk, bv, w_t, w_scale, bias, out):
    fp32, bf16 = mybir.dt.float32, mybir.dt.bfloat16
    u8, u16, u32 = mybir.dt.uint8, mybir.dt.uint16, mybir.dt.uint32
    ALU, ACT, AX = mybir.AluOpType, mybir.ActivationFunctionType, mybir.AxisListType

    stack = ExitStack()
    with stack:
        def sb(name, shape, dt=fp32):
            return stack.enter_context(nc.sbuf_tensor(name, shape, dt))

        def ps(name, shape, dt=fp32):
            return stack.enter_context(nc.psum_tensor(name, shape, dt))

        def sem(name):
            return stack.enter_context(nc.semaphore(name))

        ident = sb("ident", [128, 128])
        ident_b = sb("ident_b", [128, 128], bf16)
        wq_ts = sb("wq_ts", [128, XC, DX])
        wk_ts = sb("wk_ts", [128, XC, DC])
        bq_s = sb("bq_s", [128, XC])
        neg_one = sb("neg_one", [Q, 2])
        wqk = sb("wqk", [128, XC, DC])
        bqk = sb("bqk", [128, 1])
        wv_s = sb("wv_s", [128, DX])
        bv_b = sb("bv_b", [Q, DX])
        bias_b = sb("bias_b", [Q, DX])
        ws_s = sb("ws_s", [Q, 1])
        ws448 = sb("ws448", [Q, 1])
        eps_s = sb("eps_s", [Q, 1])
        w8 = sb("w8", [128, XC, DX], u8)
        w_bits = sb("w_bits", [128, XC, DX], u32)
        w_mag = sb("w_mag", [128, XC, DX], u32)
        w_sub = sb("w_sub", [128, XC, DX])
        w_abs = sb("w_abs", [128, XC, DX])
        w_sign = sb("w_sign", [128, XC, DX], u32)
        w_b = sb("w_b", [128, XC, DX], bf16)

        def two(name, shape, dt=fp32):
            return [sb(f"{name}_{i}", shape, dt) for i in range(2)]

        x_s = two("x_s", [Q, 2, DX])
        stats_1 = two("stats_1", [Q, 2, 6])
        moments_1 = two("moments_1", [Q, 2, 2])
        log_var_1 = two("log_var_1", [Q, 2])
        rstd_1 = two("rstd_1", [Q, 2])
        neg_mean_1 = two("neg_mean_1", [Q, 2])
        xn = two("xn", [Q, 2, DX])
        xn_t = two("xn_t", [128, XC, 2 * Q])
        tq_t = two("tq_t", [DC, 2, Q])
        xb = two("xb", [Q, 2, DX])
        x1 = two("x1", [Q, 2, DX])
        x1b = two("x1b", [Q, 2, DX])
        sum_2 = two("sum_2", [Q, 2])
        neg_mean_2 = two("neg_mean_2", [Q, 2])
        xc = two("xc", [Q, 2, DX])
        square_sum = two("square_sum", [Q, 2])
        log_var_2 = two("log_var_2", [Q, 2])
        rstd_2 = two("rstd_2", [Q, 2])
        abs_max = two("abs_max", [Q, 2])
        h_max = two("h_max", [Q, 2])
        h_floored = two("h_floored", [Q, 2])
        h_inv = two("h_inv", [Q, 2])
        q_scale = two("q_scale", [Q, 2])
        q_scale20 = two("q_scale20", [Q, 2])
        out_scale = two("out_scale", [Q, 2])
        scaled = two("scaled", [Q, 2, DX], bf16)
        power = two("power", [Q, 2, DX], bf16)
        magic = two("magic", [Q, 2, DX], bf16)
        shifted = two("shifted", [Q, 2, DX])
        quant = two("quant", [Q, 2, DX], bf16)
        quant_t = two("quant_t", [128, XC, 2, Q], bf16)
        out_s = two("out_s", [Q, 2, DX])

        ctx_s = [sb(f"ctx_s{i}", [KP, KJ, DC]) for i in range(4)]
        ctx_ts = [sb(f"ctx_ts{i}", [DC, K]) for i in range(4)]
        neg_max = sb("neg_max", [Q, 4])
        row_sum = sb("row_sum", [Q, 4])
        row_inv = sb("row_inv", [Q, 4])
        probs = two("probs", [Q, K])
        probs_t = two("probs_t", [KP, KJ, Q])
        pc_t = two("pc_t", [DC, Q])
        squares = sb("squares", [Q, DX])

        ps_x = ps("ps_x", [128, 512])
        ps_s = [ps(f"ps_s{i}", [128, 512]) for i in range(2)]
        ps_p = ps("ps_p", [128, 512])
        ps_o = [ps(f"ps_o{i}", [128, 512]) for i in range(2)]
        ps_q = ps("ps_q", [128, 1024], bf16)
        ps_f = ps("ps_f", [128, 512])

        wqk_in, wv_in, rows_in, w8_in = sem("wqk_in"), sem("wv_in"), sem("rows_in"), sem("w8_in")
        x_in = [sem(f"x_in{i}") for i in range(2)]
        ctx_in = [sem(f"ctx_in{i}") for i in range(4)]
        ctx_t_in = [sem(f"ctx_t_in{i}") for i in range(4)]
        stored = [sem(f"stored{i}") for i in range(2)]
        ident_set, ident_ready, wqk_made, wqk_ready = sem("ident_set"), sem("ident_ready"), sem("wqk_made"), sem("wqk_ready")
        eps_ready, ws_ready, w_step, neg_one_ready = sem("eps_ready"), sem("ws_ready"), sem("w_step"), sem("neg_one_ready")

        pool_passed, dve_passed = sem("pool_passed"), sem("dve_passed")

        counted = {"dve": [], "act": [], "pool": [], "pe": []}

        def counting(engine, name, per=1):
            counted[engine].append((sem(name), per))
            return counted[engine][-1][0]

        def start_counts(engine, name):
            for s, per in counted[name]:
                engine.sem_inc(s, PAST * per)

        stats_ready = counting("dve", "stats_ready")
        moments_ready = counting("dve", "moments_ready")
        max_ready = counting("dve", "max_ready", 2)
        inv_ready = counting("dve", "inv_ready", 2)
        x1_ready = counting("dve", "x1_ready", 2)
        neg_mean_2_ready = counting("dve", "neg_mean_2_ready")
        abs_max_ready = counting("dve", "abs_max_ready")
        h_max_ready = counting("dve", "h_max_ready")
        h_floored_ready = counting("dve", "h_floored_ready")
        out_scale_ready = counting("dve", "out_scale_ready")
        h_inv_ready = counting("dve", "h_inv_ready")
        q_scales_ready = counting("dve", "q_scales_ready")
        scaled_ready = counting("dve", "scaled_ready")
        power_ready = counting("dve", "power_ready")
        magic_ready = counting("dve", "magic_ready")
        shifted_ready = counting("dve", "shifted_ready")
        out_ready = counting("dve", "out_ready", 2)
        log_var_1_ready = counting("act", "log_var_1_ready")
        rstd_1_ready = counting("act", "rstd_1_ready")
        xt_ready = counting("act", "xt_ready")
        tq_ready = counting("act", "tq_ready")
        probs_ready = counting("act", "probs_ready", 2)
        probs_t_ready = counting("act", "probs_t_ready", 2)
        pc_ready = counting("act", "pc_ready", 2)
        xc_ready = counting("act", "xc_ready", 2)
        square_sum_ready = counting("act", "square_sum_ready", 2)
        log_var_2_ready = counting("act", "log_var_2_ready")
        rstd_2_ready = counting("act", "rstd_2_ready")
        quant_t_ready = counting("act", "quant_t_ready")
        neg_mean_1_ready = counting("pool", "neg_mean_1_ready")
        xn_ready = counting("pool", "xn_ready")
        xb_ready = counting("pool", "xb_ready")
        x1b_ready = counting("pool", "x1b_ready")
        quant_ready = counting("pool", "quant_ready")
        xt_made = counting("pe", "xt_made")
        tq_made = counting("pe", "tq_made")
        scores_made = counting("pe", "scores_made", 2)
        probs_t_made = counting("pe", "probs_t_made", 2)
        pc_made = counting("pe", "pc_made", 2)
        attn_made = counting("pe", "attn_made", 2)
        quant_t_made = counting("pe", "quant_t_made")
        linear_made = counting("pe", "linear_made")

        ctx_rows = ctx.rearrange("b (p j) d -> b p j d", j=KJ)
        x_rows = x.rearrange("(n h) q d -> n q h d", h=2)
        out_rows = out.rearrange("(n h) q d -> n q h d", h=2)
        KP0 = 112
        LAST_LAG = 4

        def pipeline(engine, steps):
            for u in range(LAST_LAG):
                steps(Pair(0, u))
            with engine.Fori(LAST_LAG // 2, PAIRS // 2) as half:
                steps(Pair(half, 0))
                steps(Pair(half, 1))
            for u in range(PAIRS, PAIRS + LAST_LAG):
                steps(Pair(0, u))

        def run(stage, p, *h):
            if p.exists():
                stage(p, *h)

        block = stack.enter_context(nc.Block())

        @block.sync
        def _(sp):
            def load_x(p):
                sp.wait_ge(xn_ready, count(p.back(2)))
                sp.wait_ge(xb_ready, count(p.back(2)))
                sp.dma_start(x_s[p.side][:], x_rows[p.n]).then_inc(x_in[p.side], 16)

            def load_ctx_t(p, h):
                slot = 2 * p.side + h
                sp.wait_ge(scores_made, count(p.back(2), 2, h))
                sp.dma_start(ctx_ts[slot][:], ctx_t[2 * p.n + h]).then_inc(ctx_t_in[slot], 16)

            def load_ctx(p, h):
                slot = 2 * p.side + h
                sp.wait_ge(pc_made, count(p.back(2), 2, h))
                sp.dma_start(ctx_s[slot][0:KP0], ctx_rows[2 * p.n + h, 0:KP0]).then_inc(ctx_in[slot], 16)
                sp.dma_start(ctx_s[slot][KP0:KP], ctx_rows[2 * p.n + h, KP0:KP]).then_inc(ctx_in[slot], 16)

            def store(p):
                sp.wait_ge(out_ready, count(p, 2))
                sp.dma_start(out_rows[p.n], out_s[p.side][:]).then_inc(stored[p.side], 16)

            def loads(p):
                load_x(p)
                for h in range(2):
                    load_ctx_t(p, h)
                    load_ctx(p, h)

            first, second = Pair(0, 0), Pair(0, 1)
            load_x(first)
            sp.dma_start(wq_ts[:], wq_t.rearrange("(c p) n -> p c n", p=128)).then_inc(wqk_in, 16)
            sp.dma_start(wk_ts[:], wk_t.rearrange("(c p) n -> p c n", p=128)).then_inc(wqk_in, 16)
            sp.dma_start(bq_s[:], bq).then_inc(wqk_in, 16)
            sp.dma_start(bv_b[:], bv.rearrange("(a n) -> a n", a=1).broadcast_to([Q, DX])).then_inc(rows_in, 16)
            load_ctx_t(first, 0)
            load_ctx_t(first, 1)
            load_ctx(first, 0)
            load_ctx(first, 1)
            load_x(second)
            sp.dma_start(wv_s[:], wv).then_inc(wv_in, 16)
            sp.dma_start(w8[:], w_t.rearrange("(c p) n -> p c n", p=128)).then_inc(w8_in, 16)
            sp.dma_start(bias_b[:], bias.rearrange("(a n) -> a n", a=1).broadcast_to([Q, DX])).then_inc(rows_in, 16)
            sp.dma_start(ws_s[:], w_scale.broadcast_to([Q, 1])).then_inc(rows_in, 16)
            for h in range(2):
                load_ctx_t(second, h)
                load_ctx(second, h)
            for n in (2, 3):
                loads(Pair(0, n))
            with sp.Fori(2, PAIRS // 2) as half:
                for k in range(2):
                    loads(Pair(half, k))
                    store(Pair(half, k).back(4))
            for n in range(PAIRS - 4, PAIRS):
                store(Pair(0, n))
            for i in range(2):
                sp.wait_ge(stored[i], 16 * (1 + PAIRS // 2))

        @block.gpsimd
        def _(pool):
            def negate_mean_1(p):
                pool.wait_ge(rstd_1_ready, count(p))
                pool.wait_ge(moments_ready, count(p))
                pool.wait_ge(xt_made, count(p.back(2)))
                pool.tensor_tensor(neg_mean_1[p.side][:], moments_1[p.side][:, :, 0], neg_one[:],
                                   ALU.mult).then_inc(neg_mean_1_ready, 1)

            def normalise_1(p):
                pool.wait_ge(neg_mean_1_ready, count(p))
                pool.sem_inc(pool_passed, 1)
                for h in range(2):
                    last = pool.tensor_scalar(xn[p.side][:, h], x_s[p.side][:, h], neg_mean_1[p.side][:, h:h + 1],
                                              rstd_1[p.side][:, h:h + 1], ALU.add, ALU.mult)
                last.then_inc(xn_ready, 1)

            def add_bv(p):
                pool.wait_ge(x_in[p.side], 16 * (p.turn + 1))
                pool.wait_ge(x1_ready, count(p.back(2), 2))
                pool.tensor_tensor(xb[p.side][:], x_s[p.side][:], bv_b[:].unsqueeze(1).broadcast_to([Q, 2, DX]),
                                   ALU.add).then_inc(xb_ready, 1)

            def add_bias(p):
                pool.wait_ge(x1_ready, count(p, 2))
                pool.wait_ge(out_ready, count(p.back(2), 2))
                pool.tensor_tensor(x1b[p.side][:], x1[p.side][:], bias_b[:].unsqueeze(1).broadcast_to([Q, 2, DX]),
                                   ALU.add).then_inc(x1b_ready, 1)

            def unshift(p):
                pool.wait_ge(shifted_ready, count(p))
                pool.wait_ge(quant_t_made, count(p.back(2)))
                pool.tensor_tensor(quant[p.side][:], shifted[p.side][:], magic[p.side][:],
                                   ALU.subtract).then_inc(quant_ready, 1)

            def steps(u):
                run(unshift, u.back(4))
                run(negate_mean_1, u)
                run(normalise_1, u)
                run(add_bias, u.back(3))
                run(add_bv, u)

            start_counts(pool, "pool")
            pool.memset(neg_one[:], -1.0).then_inc(neg_one_ready, 1)
            for m in (ident, ident_b):
                pool.memset(m[:], 0.0).then_inc(ident_set, 1)
            for n, m in enumerate((ident, ident_b)):
                pool.wait_ge(ident_set, n + 1)
                pool.affine_select(out=m[:], in_=m[:], compare_op=ALU.not_equal, fill=1.0, base=0,
                                   pattern=[[-1, 128]], channel_multiplier=1).then_inc(ident_ready, 1)
            pool.wait_ge(neg_one_ready, 1)
            pool.wait_ge(rows_in, 48)
            pipeline(pool, steps)

        @block.scalar
        def _(act):
            def take_log_1(p):
                act.wait_ge(moments_ready, count(p))
                act.activation(log_var_1[p.side][:], moments_1[p.side][:, :, 1], ACT.Ln,
                               bias=eps_s[:, 0:1]).then_inc(log_var_1_ready, 1)

            def take_rstd_1(p):
                act.wait_ge(log_var_1_ready, count(p))
                act.wait_ge(xn_ready, count(p.back(2)))
                act.activation(rstd_1[p.side][:], log_var_1[p.side][:], ACT.Exp, scale=-0.5).then_inc(rstd_1_ready, 1)

            def evict_xt(p):
                act.wait_ge(xt_made, count(p))
                act.wait_ge(tq_made, count(p.back(2)))
                act.activation(xn_t[p.side][:], ps_x[:, 0:XC * 2 * Q], ACT.Copy).then_inc(xt_ready, 1)

            def evict_tq(p):
                act.wait_ge(tq_made, count(p))
                act.wait_ge(scores_made, count(p.back(2), 2))
                act.activation(tq_t[p.side][:], ps_x[:, 0:2 * Q], ACT.Identity, bias=bqk[:, 0:1]).then_inc(tq_ready, 1)

            def exp(p, h):
                slot = 2 * p.side + h
                act.wait_ge(max_ready, count(p, 2, h))
                act.wait_ge(probs_t_made, count(p.back(1), 2, h))
                act.activation(probs[h][:], ps_s[h][0:Q, 0:K], ACT.Exp, bias=neg_max[:, slot:slot + 1],
                               accum_out=row_sum[:, slot:slot + 1]).then_inc(probs_ready, 1)

            def evict_probs_t(p, h):
                act.wait_ge(probs_t_made, count(p, 2, h))
                act.wait_ge(pc_made, count(p.back(1), 2, h))
                act.activation(probs_t[h][:], ps_p[0:KP, 0:KJ * Q], ACT.Copy).then_inc(probs_t_ready, 1)

            def evict_pc(p, h):
                act.wait_ge(pc_made, count(p, 2, h))
                act.wait_ge(attn_made, count(p.back(1), 2, h))
                act.activation(pc_t[h][:], ps_o[h][:, 0:Q], ACT.Copy).then_inc(pc_ready, 1)

            def center_2(p):
                act.wait_ge(neg_mean_2_ready, count(p))
                act.wait_ge(shifted_ready, count(p.back(2)))
                for h in range(2):
                    act.activation(xc[p.side][:, h], x1[p.side][:, h], ACT.Identity,
                                   bias=neg_mean_2[p.side][:, h:h + 1]).then_inc(xc_ready, 1)

            def sum_squares(p):
                for h in range(2):
                    act.wait_ge(xc_ready, count(p, 2, h))
                    act.wait_ge(square_sum_ready, count(p, 2, h, before=1))
                    act.activation(squares[:], xc[p.side][:, h], ACT.Square,
                                   accum_out=square_sum[p.side][:, h:h + 1]).then_inc(square_sum_ready, 1)

            def take_log_2(p):
                act.wait_ge(square_sum_ready, count(p, 2))
                act.activation(log_var_2[p.side][:], square_sum[p.side][:], ACT.Ln, bias=eps_s[:, 0:1],
                               scale=1.0 / DX).then_inc(log_var_2_ready, 1)

            def take_rstd_2(p):
                act.wait_ge(log_var_2_ready, count(p))
                act.wait_ge(q_scales_ready, count(p.back(2)))
                act.activation(rstd_2[p.side][:], log_var_2[p.side][:], ACT.Exp, scale=-0.5).then_inc(rstd_2_ready, 1)

            def evict_quant_t(p):
                act.wait_ge(quant_t_made, count(p))
                act.wait_ge(linear_made, count(p.back(2)))
                act.activation(quant_t[p.side][:], ps_q[:, 0:XC * 2 * Q], ACT.Copy).then_inc(quant_t_ready, 1)

            def steps(u):
                run(evict_pc, u.back(2), 0)
                run(take_log_2, u.back(3))
                run(take_log_1, u)
                run(evict_pc, u.back(2), 1)
                run(take_rstd_2, u.back(3))
                run(take_rstd_1, u)
                run(exp, u.back(1), 0)
                run(evict_quant_t, u.back(4))
                run(exp, u.back(1), 1)
                run(evict_probs_t, u.back(1), 0)
                run(evict_xt, u)
                run(center_2, u.back(2))
                run(evict_probs_t, u.back(1), 1)
                run(evict_tq, u)
                run(sum_squares, u.back(2))

            act.preload_act_table_set("natural_log_exp_and_others")
            start_counts(act, "act")
            act.wait_ge(wqk_made, 1)
            act.activation(wqk[:], ps_s[0][:, 0:XC * DC], ACT.Copy).then_inc(wqk_ready, 1)
            act.activation(bqk[:], ps_s[0][:, XC * DC:XC * DC + 1], ACT.Copy).then_inc(wqk_ready, 1)
            act.wait_ge(wqk_ready, 2)
            act.wait_ge(eps_ready, 1)
            pipeline(act, steps)

        @block.vector
        def _(dve):
            def take_stats_1(p):
                dve.wait_ge(x_in[p.side], 16 * (p.turn + 1))
                for h in range(2):
                    last = dve.bn_stats(stats_1[p.side][:, h], x_s[p.side][:, h])
                last.then_inc(stats_ready, 1)

            def take_moments_1(p):
                dve.wait_ge(neg_mean_1_ready, count(p.back(2)))
                dve.wait_ge(stats_ready, count(p))
                dve.sem_inc(dve_passed, 1)
                for h in range(2):
                    last = dve.bn_aggr(moments_1[p.side][:, h], stats_1[p.side][:, h])
                last.then_inc(moments_ready, 1)

            def row_max(p, h):
                slot = 2 * p.side + h
                dve.wait_ge(scores_made, count(p, 2, h))
                dve.tensor_reduce(neg_max[:, slot:slot + 1], ps_s[h][0:Q, 0:K], AX.X, ALU.max,
                                  negate=True).then_inc(max_ready, 1)

            def invert_sum(p, h):
                slot = 2 * p.side + h
                dve.wait_ge(probs_ready, count(p, 2, h))
                dve.reciprocal(row_inv[:, slot:slot + 1], row_sum[:, slot:slot + 1]).then_inc(inv_ready, 1)

            def residual_1(p, h):
                slot = 2 * p.side + h
                dve.wait_ge(attn_made, count(p, 2, h))
                dve.wait_ge(inv_ready, count(p, 2, h))
                dve.wait_ge(xb_ready, count(p))
                dve.wait_ge(xc_ready, count(p.back(2), 2))
                dve.wait_ge(x1b_ready, count(p.back(2)))
                dve.scalar_tensor_tensor(x1[p.side][:, h], ps_o[h][0:Q, DC:DC + DX], row_inv[:, slot:slot + 1],
                                         xb[p.side][:, h], ALU.mult, ALU.add,
                                         accum_out=sum_2[p.side][:, h:h + 1]).then_inc(x1_ready, 1)

            def negate_mean_2(p):
                dve.wait_ge(x1_ready, count(p, 2))
                dve.tensor_scalar(neg_mean_2[p.side][:], sum_2[p.side][:], -1.0 / DX, None,
                                  ALU.mult).then_inc(neg_mean_2_ready, 1)

            def take_abs_max(p):
                dve.wait_ge(xc_ready, count(p, 2))
                dve.tensor_reduce(abs_max[p.side][:], xc[p.side][:], AX.X, ALU.max,
                                  apply_absolute_value=True).then_inc(abs_max_ready, 1)

            def scale_max(p):
                dve.wait_ge(abs_max_ready, count(p))
                dve.wait_ge(rstd_2_ready, count(p))
                dve.tensor_tensor(h_max[p.side][:], abs_max[p.side][:], rstd_2[p.side][:],
                                  ALU.mult).then_inc(h_max_ready, 1)

            def floor_max(p):
                dve.wait_ge(h_max_ready, count(p))
                dve.tensor_scalar(h_floored[p.side][:], h_max[p.side][:], AMAX_FLOOR, None,
                                  ALU.max).then_inc(h_floored_ready, 1)

            def take_out_scale(p):
                dve.wait_ge(h_floored_ready, count(p))
                dve.wait_ge(out_ready, count(p.back(2), 2))
                dve.tensor_scalar(out_scale[p.side][:], h_floored[p.side][:], ws448[:, 0:1], None,
                                  ALU.mult).then_inc(out_scale_ready, 1)

            def invert_max(p):
                dve.wait_ge(h_floored_ready, count(p))
                dve.reciprocal(h_inv[p.side][:], h_floored[p.side][:]).then_inc(h_inv_ready, 1)

            def take_q_scales(p):
                dve.wait_ge(h_inv_ready, count(p))
                dve.scalar_tensor_tensor(q_scale[p.side][:], h_inv[p.side][:], FP8_MAX, rstd_2[p.side][:],
                                         ALU.mult, ALU.mult)
                dve.scalar_tensor_tensor(q_scale20[p.side][:], h_inv[p.side][:], FP8_MAX * 2.0 ** 20, rstd_2[p.side][:],
                                         ALU.mult, ALU.mult).then_inc(q_scales_ready, 1)

            def scale_up(p):
                dve.wait_ge(q_scales_ready, count(p))
                for h in range(2):
                    last = dve.tensor_scalar(scaled[p.side][:, h], xc[p.side][:, h], q_scale20[p.side][:, h:h + 1],
                                             None, ALU.mult)
                last.then_inc(scaled_ready, 1)

            def take_power(p):
                dve.wait_ge(scaled_ready, count(p))
                dve.tensor_scalar(power[p.side][:].bitcast(u16), scaled[p.side][:].bitcast(u16), 0x7F80, 0x0040,
                                  ALU.bitwise_and, ALU.bitwise_or).then_inc(power_ready, 1)

            def floor_power(p):
                dve.wait_ge(power_ready, count(p))
                dve.wait_ge(quant_ready, count(p.back(2)))
                dve.tensor_scalar(magic[p.side][:], power[p.side][:], 1.5 * 2.0 ** (20 - 6), None,
                                  ALU.max).then_inc(magic_ready, 1)

            def shift(p):
                dve.wait_ge(magic_ready, count(p))
                for h in range(2):
                    last = dve.scalar_tensor_tensor(shifted[p.side][:, h], xc[p.side][:, h], q_scale[p.side][:, h:h + 1],
                                                    magic[p.side][:, h], ALU.mult, ALU.add)
                last.then_inc(shifted_ready, 1)

            def residual_2(p, h):
                dve.wait_ge(linear_made, count(p))
                dve.wait_ge(x1b_ready, count(p))
                dve.wait_ge(out_scale_ready, count(p))
                dve.wait_ge(stored[p.side], 16 * (p.turn + 1))
                dve.scalar_tensor_tensor(out_s[p.side][:, h], ps_f[0:Q, h * DX:(h + 1) * DX],
                                         out_scale[p.side][:, h:h + 1], x1b[p.side][:, h],
                                         ALU.mult, ALU.add).then_inc(out_ready, 1)

            def decode_weights():
                def after(i):
                    dve.wait_ge(w_step, i)

                dve.wait_ge(w8_in, 16)
                dve.tensor_copy(w_bits[:], w8[:]).then_inc(w_step, 1)
                after(1)
                dve.tensor_scalar(w_mag[:], w_bits[:], 0x7F, 20, ALU.bitwise_and, ALU.logical_shift_left).then_inc(w_step, 1)
                dve.tensor_scalar(w_sign[:], w_bits[:], 0x80, 24, ALU.bitwise_and, ALU.logical_shift_left).then_inc(w_step, 1)
                after(2)
                dve.tensor_scalar(w_sub[:], w_mag[:], 7.0 * 2 ** 20, 2.0 ** -29, ALU.min, ALU.mult).then_inc(w_step, 1)
                after(4)
                dve.scalar_tensor_tensor(w_abs[:], w_mag[:].bitcast(fp32), 2.0 ** 120, w_sub[:],
                                         ALU.mult, ALU.max).then_inc(w_step, 1)
                after(5)
                dve.tensor_tensor(w_bits[:], w_abs[:].bitcast(u32), w_sign[:], ALU.bitwise_or).then_inc(w_step, 1)
                after(6)
                dve.tensor_copy(w_b[:], w_bits[:].bitcast(fp32)).then_inc(w_step, 1)
                dve.wait_ge(rows_in, 48)
                dve.tensor_scalar(ws448[:], ws_s[:], 1.0 / FP8_MAX, None, ALU.mult).then_inc(ws_ready, 1)
                dve.wait_ge(ws_ready, 1)

            def steps(u):
                run(take_stats_1, u)
                run(invert_sum, u.back(2), 1)
                run(take_moments_1, u)
                if not isinstance(u.half, int) or u.n != 0:
                    pass
                else:
                    decode_weights()
                run(take_abs_max, u.back(3))
                run(row_max, u.back(1), 0)
                run(scale_max, u.back(3))
                run(floor_max, u.back(3))
                run(row_max, u.back(1), 1)
                run(invert_max, u.back(3))
                run(take_out_scale, u.back(3))
                run(residual_1, u.back(2), 0)
                run(take_q_scales, u.back(3))
                run(residual_1, u.back(2), 1)
                run(scale_up, u.back(3))
                run(negate_mean_2, u.back(2))
                run(take_power, u.back(3))
                run(invert_sum, u.back(1), 0)
                run(floor_power, u.back(3))
                run(residual_2, u.back(4), 1)
                run(shift, u.back(3))
                run(residual_2, u.back(4), 0)

            start_counts(dve, "dve")
            for i in range(2):
                dve.sem_inc(stored[i], 16)
            dve.memset(eps_s[:], EPS).then_inc(eps_ready, 1)
            pipeline(dve, steps)

        @block.tensor
        def _(pe):
            def transpose_x(p):
                pe.wait_ge(xn_ready, count(p))
                pe.wait_ge(tq_ready, count(p.back(1)))
                for c in range(XC):
                    for h in range(2):
                        at = (2 * c + h) * Q
                        last = pe.transpose(ps_x[:, at:at + Q], xn[p.side][:, h, 128 * c:128 * (c + 1)], ident[0:Q, 0:Q])
                last.then_inc(xt_made, 1)

            def project(p):
                pe.wait_ge(xt_ready, count(p))
                for c in range(XC):
                    last = pe.matmul(ps_x[:, 0:2 * Q], wqk[:, c], xn_t[p.side][:, c], start=c == 0, stop=c == XC - 1)
                last.then_inc(tq_made, 1)

            def score(p, h):
                slot = 2 * p.side + h
                pe.wait_ge(tq_ready, count(p))
                pe.wait_ge(ctx_t_in[slot], 16 * (p.turn + 1))
                pe.wait_ge(probs_ready, count(p.back(1), 2, h))
                pe.matmul(ps_s[h][0:Q, 0:K], tq_t[p.side][:, h], ctx_ts[slot][:], start=True, stop=True)\
                    .then_inc(scores_made, 1)

            def transpose_probs(p, h):
                pe.wait_ge(probs_ready, count(p, 2, h))
                pe.wait_ge(probs_t_ready, count(p, 2, h, before=1))
                for j in range(KJ):
                    last = pe.transpose(ps_p[0:KP, j * Q:(j + 1) * Q], probs[h][:, j * KP:(j + 1) * KP], ident[0:Q, 0:Q])
                last.then_inc(probs_t_made, 1)

            def attend(p, h):
                slot = 2 * p.side + h
                pe.wait_ge(probs_t_ready, count(p, 2, h))
                pe.wait_ge(ctx_in[slot], 32 * (p.turn + 1))
                pe.wait_ge(x1_ready, count(p.back(1), 2, h))
                for j in range(KJ):
                    last = pe.matmul(ps_o[h][:, 0:Q], ctx_s[slot][:, j], probs_t[h][:, j], start=j == 0, stop=j == KJ - 1)
                last.then_inc(pc_made, 1)

            def value(p, h):
                pe.wait_ge(pc_ready, count(p, 2, h))
                pe.matmul(ps_o[h][0:Q, DC:DC + DX], pc_t[h][:], wv_s[:], start=True, stop=True).then_inc(attn_made, 1)

            def transpose_quant(p):
                pe.wait_ge(quant_ready, count(p))
                pe.wait_ge(quant_t_ready, count(p.back(1)))
                for c in range(XC):
                    for h in range(2):
                        at = (2 * c + h) * Q
                        last = pe.transpose(ps_q[:, at:at + Q], quant[p.side][:, h, 128 * c:128 * (c + 1)], ident_b[0:Q, 0:Q])
                last.then_inc(quant_t_made, 1)

            def linear(p):
                pe.wait_ge(quant_t_ready, count(p))
                pe.wait_ge(out_ready, count(p.back(1), 2))
                for h in range(2):
                    for c in range(XC):
                        last = pe.matmul(ps_f[0:Q, h * DX:(h + 1) * DX], quant_t[p.side][:, c, h], w_b[:, c],
                                         start=c == 0, stop=c == XC - 1)
                last.then_inc(linear_made, 1)

            def steps(u):
                run(transpose_probs, u.back(1), 0)
                run(transpose_x, u)
                run(linear, u.back(4))
                run(transpose_probs, u.back(1), 1)
                run(project, u)
                run(attend, u.back(1), 0)
                run(attend, u.back(1), 1)
                run(score, u, 0)
                run(score, u, 1)
                run(value, u.back(1), 0)
                run(transpose_quant, u.back(3))
                run(value, u.back(1), 1)

            start_counts(pe, "pe")
            pe.wait_ge(wqk_in, 48)
            for i in range(XC):
                for e in range(XC):
                    pe.matmul(ps_s[0][:, i * DC:(i + 1) * DC], wq_ts[:, e, 128 * i:128 * (i + 1)], wk_ts[:, e],
                              start=e == 0, stop=e == XC - 1)
            for e in range(XC):
                last = pe.matmul(ps_s[0][:, XC * DC:XC * DC + 1], wk_ts[:, e], bq_s[:, e:e + 1],
                                 start=e == 0, stop=e == XC - 1)
            last.then_inc(wqk_made, 1)
            pe.wait_ge(wqk_ready, 2)
            pe.wait_ge(ident_ready, 2)
            pe.wait_ge(wv_in, 16)
            pe.wait_ge(w_step, 7)
            pipeline(pe, steps)


def kernel(x, ctx_512, L0_xattn_Wq, L0_xattn_bq, L0_xattn_Wk, L0_xattn_bk, L0_xattn_Wv, L0_xattn_bv,
           L0_ffn_weight, L0_ffn_weight_scale, L0_ffn_bias):
    import numpy as np
    import concourse.bacc as bacc
    from concourse.bass_utils import run_bass_kernel_spmd

    ctx = np.asarray(ctx_512)
    arrays = {
        "x": np.asarray(x),
        "ctx": ctx,
        "ctx_t": ctx.reshape(B, KP, KJ, DC).transpose(0, 3, 2, 1).reshape(B, DC, K),
        "wq_t": np.asarray(L0_xattn_Wq).T,
        "wk_t": np.asarray(L0_xattn_Wk).T,
        "wv": np.asarray(L0_xattn_Wv),
        "bq": np.asarray(L0_xattn_bq).reshape(XC, 128).T,
        "bk": np.asarray(L0_xattn_bk),
        "bv": np.asarray(L0_xattn_bv),
        "w_t": np.asarray(L0_ffn_weight).T.view(np.uint8),
        "w_scale": np.asarray(L0_ffn_weight_scale).reshape(1, 1),
        "bias": np.asarray(L0_ffn_bias),
    }
    arrays = {f"in_{k}": np.ascontiguousarray(v) for k, v in arrays.items()}
    nc = bacc.Bacc("TRN2", target_bir_lowering=False, num_devices=1)
    args = [nc.dram_tensor(k, v.shape, mybir.dt.from_np(v.dtype), kind="ExternalInput").ap() for k, v in arrays.items()]
    args.append(nc.dram_tensor("out_0", (B, Q, DX), mybir.dt.float32, kind="ExternalOutput").ap())
    xattn_ffn_kernel(nc, *args)
    return run_bass_kernel_spmd(nc, [arrays], core_ids=[0]).results[0]["out_0"]
```

```python
import concourse.bass as bass
from concourse import mybir
from contextlib import ExitStack

B, Q, DX = 16, 112, 256
K, DC = 375, 128
KP, KJ = 125, 3
PAIRS = B // 2
XC = DX // 128
FP8_MAX = 448.0
EPS = 1e-5
AMAX_FLOOR = 1e-12

PAST = 2
GROUPS = (range(0, 1), range(1, 2), range(2, 5), range(5, PAIRS))
ALONE = 2


def pairs_in(g):
    return slice(GROUPS[g].start, GROUPS[g].stop)


def groups_with(p):
    return sum(1 for pairs in GROUPS if not isinstance(p.half, int) or pairs.start <= p.n)


class Pair:

    def __init__(self, half, k):
        self.half, self.k = half, k

    def back(self, pairs):
        return Pair(self.half, self.k - pairs)

    @property
    def n(self):
        return 2 * self.half + self.k

    @property
    def side(self):
        return self.k % 2

    @property
    def turn(self):
        return self.half + self.k // 2

    def exists(self):
        return not isinstance(self.half, int) or 0 <= self.n < PAIRS


def count(p, per=1, h=None, before=0):
    return 2 * per * p.half + (per * (p.k + PAST) + (per if h is None else h + 1) - before)


def xattn_ffn_kernel(nc, x, ctx, ctx_t, wq_t, wk_t, wv, bq, bv, w_t, w_scale, bias, out):
    fp32, bf16 = mybir.dt.float32, mybir.dt.bfloat16
    u8, u16, u32 = mybir.dt.uint8, mybir.dt.uint16, mybir.dt.uint32
    ALU, ACT, AX = mybir.AluOpType, mybir.ActivationFunctionType, mybir.AxisListType

    stack = ExitStack()
    with stack:
        def sb(name, shape, dt=fp32):
            return stack.enter_context(nc.sbuf_tensor(name, shape, dt))

        def ps(name, shape, dt=fp32):
            return stack.enter_context(nc.psum_tensor(name, shape, dt))

        def sem(name):
            return stack.enter_context(nc.semaphore(name))

        ident = sb("ident", [128, 128])
        ident_b = sb("ident_b", [128, 128], bf16)
        warm = sb("warm", [128, 512], bf16)
        wq_ts = sb("wq_ts", [128, XC, DX])
        wk_ts = sb("wk_ts", [128, XC, DC])
        bq_s = sb("bq_s", [128, XC])
        neg_one = sb("neg_one", [Q, 2])
        neg_share = sb("neg_share", [Q, 2])
        wqk = sb("wqk", [128, XC, DC])
        bqk = sb("bqk", [128, 1])
        wv_s = sb("wv_s", [128, DX])
        bv_b = sb("bv_b", [Q, DX])
        bias_b = sb("bias_b", [Q, DX])
        ws_s = sb("ws_s", [Q, 1])
        ws448 = sb("ws448", [Q, 1])
        eps_s = sb("eps_s", [Q, 1])
        w8 = sb("w8", [128, XC, DX], u8)
        w_bits = sb("w_bits", [128, XC, DX], u32)
        w_mag = sb("w_mag", [128, XC, DX], u32)
        w_sub = sb("w_sub", [128, XC, DX])
        w_abs = sb("w_abs", [128, XC, DX])
        w_sign = sb("w_sign", [128, XC, DX], u32)
        w_b = sb("w_b", [128, XC, DX], bf16)

        x_ahead = sb("x_ahead", [Q, PAIRS - ALONE, 2, DX])
        stats_1 = sb("stats_1", [Q, PAIRS, 2, 6])
        moments_1 = sb("moments_1", [Q, PAIRS, 2, 2])
        log_var_1 = sb("log_var_1", [Q, PAIRS, 2])

        def two(name, shape, dt=fp32):
            return [sb(f"{name}_{i}", shape, dt) for i in range(2)]

        x_s = two("x_s", [Q, 2, DX])
        rstd_1 = two("rstd_1", [Q, 2])
        neg_mean_1 = two("neg_mean_1", [Q, 2])
        xn = two("xn", [Q, 2, DX])
        xn_t = two("xn_t", [128, XC, 2 * Q])
        tq_t = two("tq_t", [DC, 2, Q])
        xb = two("xb", [Q, 2, DX])
        x1 = two("x1", [Q, 2, DX])
        x1b = two("x1b", [Q, 2, DX])
        sum_2 = two("sum_2", [Q, 2])
        neg_mean_2 = two("neg_mean_2", [Q, 2])
        xc = two("xc", [Q, 2, DX])
        square_sum = two("square_sum", [Q, 2])
        log_var_2 = two("log_var_2", [Q, 2])
        rstd_2 = two("rstd_2", [Q, 2])
        abs_max = two("abs_max", [Q, 2])
        h_max = two("h_max", [Q, 2])
        h_inv = two("h_inv", [Q, 2])
        h_floored = two("h_floored", [Q, 2])
        q_scale = two("q_scale", [Q, 2])
        out_scale = two("out_scale", [Q, 2])
        scaled = two("scaled", [Q, 2, DX], bf16)
        power = two("power", [Q, 2, DX], bf16)
        magic = two("magic", [Q, 2, DX], bf16)
        shifted = two("shifted", [Q, 2, DX])
        quant = two("quant", [Q, 2, DX], bf16)
        quant_t = two("quant_t", [128, XC, 2, Q], bf16)
        out_s = two("out_s", [Q, 2, DX])

        ctx_s = two("ctx_s", [KP, 2, KJ, DC])
        ctx_ts = two("ctx_ts", [DC, 2, K])

        neg_max = sb("neg_max", [Q, 4])
        row_sum = sb("row_sum", [Q, 4])
        row_inv = sb("row_inv", [Q, 4])
        probs = two("probs", [Q, K])
        probs_t = two("probs_t", [KP, KJ, Q])
        pc_t = two("pc_t", [DC, Q])
        squares = sb("squares", [Q, DX])

        ps_x = ps("ps_x", [128, 512])
        ps_s = [ps(f"ps_s{i}", [128, 512]) for i in range(2)]
        ps_p = ps("ps_p", [128, 512])
        ps_o = [ps(f"ps_o{i}", [128, 512]) for i in range(2)]
        ps_q = ps("ps_q", [128, 1024], bf16)
        ps_f = ps("ps_f", [128, 512])

        wqk_in, wv_in, w8_in = sem("wqk_in"), sem("wv_in"), sem("w8_in")
        bv_in, bias_in, ws_in = sem("bv_in"), sem("bias_in"), sem("ws_in")
        x_in = [sem(f"x_in{i}") for i in range(2)]
        x_ahead_in = [sem(f"x_ahead_in{i}") for i in range(len(GROUPS) - ALONE)]
        stats_ready, moments_ready = sem("stats_ready"), sem("moments_ready")
        log_var_1_ready = sem("log_var_1_ready")
        ctx_in = [sem(f"ctx_in{i}") for i in range(2)]
        ctx_t_in = [sem(f"ctx_t_in{i}") for i in range(2)]
        stored = [sem(f"stored{i}") for i in range(2)]
        ident_set, ident_ready, wqk_made, wqk_ready = sem("ident_set"), sem("ident_ready"), sem("wqk_made"), sem("wqk_ready")
        eps_ready, ws_ready, w_step, neg_one_ready = sem("eps_ready"), sem("ws_ready"), sem("w_step"), sem("neg_one_ready")

        warm_set, second_quant_ready = sem("warm_set"), sem("second_quant_ready")
        pool_passed = sem("pool_passed")

        counted = {"dve": [], "act": [], "pool": [], "pe": []}

        def counting(engine, name, per=1):
            counted[engine].append((sem(name), per))
            return counted[engine][-1][0]

        def start_counts(engine, name):
            for s, per in counted[name]:
                engine.sem_inc(s, PAST * per)

        max_ready = counting("dve", "max_ready", 2)
        inv_ready = counting("dve", "inv_ready")
        x1_ready = counting("dve", "x1_ready", 2)
        abs_max_ready = counting("dve", "abs_max_ready")
        h_inv_ready = counting("dve", "h_inv_ready")
        h_max_ready = counting("dve", "h_max_ready")
        h_floored_ready = counting("dve", "h_floored_ready")
        q_scale_ready = counting("dve", "q_scale_ready")
        scaled_0_ready = counting("dve", "scaled_0_ready")
        power_ready = counting("dve", "power_ready")
        magic_ready = counting("dve", "magic_ready")
        shifted_ready = counting("dve", "shifted_ready", 2)
        out_ready = counting("dve", "out_ready", 2)
        rstd_1_ready = counting("act", "rstd_1_ready")
        xt_ready = counting("act", "xt_ready")
        tq_ready = counting("act", "tq_ready")
        probs_ready = counting("act", "probs_ready", 2)
        probs_t_ready = counting("act", "probs_t_ready", 2)
        pc_ready = counting("act", "pc_ready", 2)
        xc_ready = counting("act", "xc_ready", 2)
        square_sum_ready = counting("act", "square_sum_ready", 2)
        log_var_2_ready = counting("act", "log_var_2_ready")
        rstd_2_ready = counting("act", "rstd_2_ready")
        scaled_1_ready = counting("act", "scaled_1_ready")
        quant_t_ready = counting("act", "quant_t_ready")
        neg_mean_1_ready = counting("pool", "neg_mean_1_ready")
        neg_mean_2_ready = counting("pool", "neg_mean_2_ready")
        out_scale_ready = counting("pool", "out_scale_ready")
        xn_ready = counting("pool", "xn_ready")
        xb_ready = counting("pool", "xb_ready")
        x1b_ready = counting("pool", "x1b_ready")
        quant_ready = counting("pool", "quant_ready")
        xt_made = counting("pe", "xt_made")
        tq_made = counting("pe", "tq_made")
        scores_made = counting("pe", "scores_made", 2)
        probs_t_made = counting("pe", "probs_t_made", 2)
        pc_made = counting("pe", "pc_made", 2)
        attn_made = counting("pe", "attn_made", 2)
        quant_t_made = counting("pe", "quant_t_made")
        linear_made = counting("pe", "linear_made")

        ctx_rows = ctx.rearrange("(n h) (p j) d -> n p h j d", h=2, j=KJ)
        ctx_cols = ctx_t.rearrange("(n h) d k -> n d h k", h=2)
        x_rows = x.rearrange("(n h) q d -> n q h d", h=2)
        x_all = x.rearrange("(n h) q d -> q n h d", h=2)
        out_rows = out.rearrange("(n h) q d -> n q h d", h=2)
        KP0 = 112
        LAST_LAG = 4

        def pipeline(engine, steps):
            for u in range(LAST_LAG):
                steps(Pair(0, u))
            with engine.Fori(LAST_LAG // 2, PAIRS // 2) as half:
                steps(Pair(half, 0))
                steps(Pair(half, 1))
            for u in range(PAIRS, PAIRS + LAST_LAG):
                steps(Pair(0, u))

        def in_step(u, n):
            return isinstance(u.half, int) and u.n == n

        def is_last(p):
            return isinstance(p.half, int) and p.n == PAIRS - 1

        def run(stage, p, *h):
            if p.exists():
                stage(p, *h)

        block = stack.enter_context(nc.Block())

        @block.sync
        def _(sp):
            def load_x(p):
                sp.wait_ge(xn_ready, count(p.back(2)))
                sp.wait_ge(xb_ready, count(p.back(2)))
                sp.dma_start(x_s[p.side][:], x_rows[p.n]).then_inc(x_in[p.side], 16)

            def load_ctx_t(p):
                sp.wait_ge(scores_made, count(p.back(2), 2))
                sp.dma_start(ctx_ts[p.side][:], ctx_cols[p.n]).then_inc(ctx_t_in[p.side], 16)

            def load_ctx(p):
                sp.wait_ge(pc_made, count(p.back(2), 2))
                sp.dma_start(ctx_s[p.side][0:KP0], ctx_rows[p.n, 0:KP0]).then_inc(ctx_in[p.side], 16)
                sp.dma_start(ctx_s[p.side][KP0:KP], ctx_rows[p.n, KP0:KP]).then_inc(ctx_in[p.side], 16)

            def load_x_ahead(g):
                pairs = GROUPS[g]
                sp.dma_start(x_ahead[:, pairs.start - ALONE:pairs.stop - ALONE], x_all[:, pairs.start:pairs.stop])\
                    .then_inc(x_ahead_in[g - ALONE], 16)

            def store(p):
                sp.wait_ge(out_ready, count(p, 2))
                sp.dma_start(out_rows[p.n], out_s[p.side][:]).then_inc(stored[p.side], 16)

            def loads(p):
                load_x(p)
                load_ctx_t(p)
                load_ctx(p)

            first, second = Pair(0, 0), Pair(0, 1)
            load_x(first)
            sp.dma_start(wk_ts[:], wk_t.rearrange("(c p) n -> p c n", p=128)).then_inc(wqk_in, 16)
            sp.dma_start(wq_ts[:], wq_t.rearrange("(c p) n -> p c n", p=128)).then_inc(wqk_in, 16)
            sp.dma_start(bq_s[:], bq).then_inc(wqk_in, 16)
            load_x(second)
            load_ctx_t(first)
            sp.dma_start(w8[:], w_t.rearrange("(c p) n -> p c n", p=128)).then_inc(w8_in, 16)
            sp.dma_start(bv_b[:], bv.rearrange("(a n) -> a n", a=1).broadcast_to([Q, DX])).then_inc(bv_in, 16)
            load_ctx(first)
            sp.dma_start(wv_s[:], wv).then_inc(wv_in, 16)
            load_x_ahead(ALONE)
            load_ctx_t(second)
            load_ctx(second)
            load_x_ahead(ALONE + 1)
            sp.dma_start(bias_b[:], bias.rearrange("(a n) -> a n", a=1).broadcast_to([Q, DX])).then_inc(bias_in, 16)
            sp.dma_start(ws_s[:], w_scale.broadcast_to([Q, 1])).then_inc(ws_in, 16)
            with sp.Fori(1, PAIRS // 2 - 1) as half:
                for k in range(2):
                    loads(Pair(half, k))
            for k in range(2):
                loads(Pair(0, PAIRS - 2 + k))
                store(Pair(0, k))
            with sp.Fori(1, PAIRS // 2) as half:
                for k in range(2):
                    store(Pair(half, k))
            for i in range(2):
                sp.wait_ge(stored[i], 16 * (1 + PAIRS // 2))

        @block.gpsimd
        def _(pool):
            def negate_mean_1(p):
                pool.wait_ge(rstd_1_ready, count(p))
                pool.wait_ge(moments_ready, groups_with(p))
                pool.wait_ge(xt_made, count(p.back(2)))
                pool.wait_ge(x_in[p.side], 16 * (p.turn + 1))
                pool.tensor_tensor(neg_mean_1[p.side][:], moments_1[:, p.n, :, 0], neg_one[:],
                                   ALU.mult).then_inc(neg_mean_1_ready, 1)

            def normalise_1(p):
                pool.wait_ge(neg_mean_1_ready, count(p))
                pool.sem_inc(pool_passed, 1)
                for h in range(2):
                    last = pool.tensor_scalar(xn[p.side][:, h], x_s[p.side][:, h], neg_mean_1[p.side][:, h:h + 1],
                                              rstd_1[p.side][:, h:h + 1], ALU.add, ALU.mult)
                last.then_inc(xn_ready, 1)

            def add_bv(p):
                pool.wait_ge(bv_in, 16)
                pool.wait_ge(x_in[p.side], 16 * (p.turn + 1))
                pool.wait_ge(x1_ready, count(p.back(2), 2))
                pool.tensor_tensor(xb[p.side][:], x_s[p.side][:], bv_b[:].unsqueeze(1).broadcast_to([Q, 2, DX]),
                                   ALU.add).then_inc(xb_ready, 1)

            def add_bias(p):
                pool.wait_ge(bias_in, 16)
                pool.wait_ge(x1_ready, count(p, 2))
                pool.wait_ge(out_ready, count(p.back(2), 2))
                pool.tensor_tensor(x1b[p.side][:], x1[p.side][:], bias_b[:].unsqueeze(1).broadcast_to([Q, 2, DX]),
                                   ALU.add).then_inc(x1b_ready, 1)

            def negate_mean_2(p):
                pool.wait_ge(x1_ready, count(p, 2))
                pool.wait_ge(xc_ready, count(p.back(2), 2))
                pool.tensor_tensor(neg_mean_2[p.side][:], sum_2[p.side][:], neg_share[:],
                                   ALU.mult).then_inc(neg_mean_2_ready, 1)

            def take_out_scale(p):
                pool.wait_ge(ws_ready, 1)
                pool.wait_ge(h_floored_ready, count(p))
                pool.wait_ge(out_ready, count(p.back(2), 2))
                pool.tensor_tensor(out_scale[p.side][:], h_floored[p.side][:], ws448[:].broadcast_to([Q, 2]),
                                   ALU.mult).then_inc(out_scale_ready, 1)

            def unshift(p):
                batches = 1 if is_last(p) else 2
                pool.wait_ge(shifted_ready, count(p, 2, batches - 1))
                pool.wait_ge(quant_t_made, count(p.back(2)))
                pool.tensor_tensor(quant[p.side][:, 0:batches], shifted[p.side][:, 0:batches],
                                   magic[p.side][:, 0:batches], ALU.subtract).then_inc(quant_ready, 1)

            def steps(u):
                run(take_out_scale, u.back(4))
                run(negate_mean_2, u.back(3))
                run(add_bv, u.back(1))
                run(negate_mean_1, u)
                run(normalise_1, u)
                run(unshift, u.back(4))
                run(add_bias, u.back(3))

            start_counts(pool, "pool")
            pool.memset(neg_one[:], -1.0).then_inc(neg_one_ready, 1)
            pool.memset(neg_share[:], -1.0 / DX).then_inc(neg_one_ready, 1)
            for m in (ident, ident_b):
                pool.memset(m[:], 0.0).then_inc(ident_set, 1)
            for n, m in enumerate((ident, ident_b)):
                pool.wait_ge(ident_set, n + 1)
                pool.affine_select(out=m[:], in_=m[:], compare_op=ALU.not_equal, fill=1.0, base=0,
                                   pattern=[[-1, 128]], channel_multiplier=1).then_inc(ident_ready, 1)
            pool.wait_ge(neg_one_ready, 2)
            pipeline(pool, steps)

        @block.scalar
        def _(act):
            def take_log_1(g):
                act.wait_ge(moments_ready, g + 1)
                act.activation(log_var_1[:, pairs_in(g)], moments_1[:, pairs_in(g), :, 1], ACT.Ln,
                               bias=eps_s[:, 0:1]).then_inc(log_var_1_ready, 1)

            def take_rstd_1(p):
                act.wait_ge(log_var_1_ready, groups_with(p))
                act.wait_ge(xn_ready, count(p.back(2)))
                act.activation(rstd_1[p.side][:], log_var_1[:, p.n], ACT.Exp, scale=-0.5).then_inc(rstd_1_ready, 1)

            def evict_wqk():
                act.wait_ge(wqk_made, 1)
                act.activation(wqk[:], ps_s[0][:, 0:XC * DC], ACT.Copy).then_inc(wqk_ready, 1)
                act.wait_ge(wqk_made, 2)
                act.activation(bqk[:], ps_s[1][:, 0:1], ACT.Copy).then_inc(wqk_ready, 1)
                act.wait_ge(wqk_ready, 2)

            def evict_xt(p):
                act.wait_ge(xt_made, count(p))
                act.wait_ge(tq_made, count(p.back(2)))
                act.activation(xn_t[p.side][:], ps_x[:, 0:XC * 2 * Q], ACT.Copy).then_inc(xt_ready, 1)

            def evict_tq(p):
                act.wait_ge(tq_made, count(p))
                act.wait_ge(scores_made, count(p.back(2), 2))
                act.activation(tq_t[p.side][:], ps_x[:, 0:2 * Q], ACT.Identity, bias=bqk[:, 0:1]).then_inc(tq_ready, 1)

            def exp(p, h):
                slot = 2 * p.side + h
                act.wait_ge(max_ready, count(p, 2, h))
                act.wait_ge(probs_t_made, count(p.back(1), 2, h))
                act.activation(probs[h][:], ps_s[h][0:Q, 0:K], ACT.Exp, bias=neg_max[:, slot:slot + 1],
                               accum_out=row_sum[:, slot:slot + 1]).then_inc(probs_ready, 1)

            def evict_probs_t(p, h):
                act.wait_ge(probs_t_made, count(p, 2, h))
                act.wait_ge(pc_made, count(p.back(1), 2, h))
                act.activation(probs_t[h][:], ps_p[0:KP, 0:KJ * Q], ACT.Copy).then_inc(probs_t_ready, 1)

            def evict_pc(p, h):
                act.wait_ge(pc_made, count(p, 2, h))
                act.wait_ge(attn_made, count(p.back(1), 2, h))
                act.activation(pc_t[h][:], ps_o[h][:, 0:Q], ACT.Copy).then_inc(pc_ready, 1)

            def center_2(p):
                act.wait_ge(neg_mean_2_ready, count(p))
                act.wait_ge(shifted_ready, count(p.back(2), 2))
                for h in range(2):
                    act.activation(xc[p.side][:, h], x1[p.side][:, h], ACT.Identity,
                                   bias=neg_mean_2[p.side][:, h:h + 1]).then_inc(xc_ready, 1)

            def sum_squares(p):
                for h in range(2):
                    act.wait_ge(xc_ready, count(p, 2, h))
                    act.wait_ge(square_sum_ready, count(p, 2, h, before=1))
                    act.activation(squares[:], xc[p.side][:, h], ACT.Square,
                                   accum_out=square_sum[p.side][:, h:h + 1]).then_inc(square_sum_ready, 1)

            def take_log_2(p):
                act.wait_ge(square_sum_ready, count(p, 2))
                act.activation(log_var_2[p.side][:], square_sum[p.side][:], ACT.Ln, bias=eps_s[:, 0:1],
                               scale=1.0 / DX).then_inc(log_var_2_ready, 1)

            def take_rstd_2(p):
                act.wait_ge(log_var_2_ready, count(p))
                act.wait_ge(q_scale_ready, count(p.back(2)))
                act.activation(rstd_2[p.side][:], log_var_2[p.side][:], ACT.Exp, scale=-0.5).then_inc(rstd_2_ready, 1)

            def scale_up_1(p):
                act.wait_ge(q_scale_ready, count(p))
                act.wait_ge(power_ready, count(p.back(2)))
                act.activation(scaled[p.side][:, 1], xc[p.side][:, 1], ACT.Copy,
                               scale=q_scale[p.side][:, 1:2]).then_inc(scaled_1_ready, 1)

            def evict_quant_t(p):
                act.wait_ge(quant_t_made, count(p))
                act.wait_ge(linear_made, count(p.back(2)))
                act.activation(quant_t[p.side][:], ps_q[:, 0:XC * 2 * Q], ACT.Copy).then_inc(quant_t_ready, 1)

            def steps(u):
                if in_step(u, 0):
                    take_log_1(0)
                run(take_rstd_1, u)
                run(center_2, u.back(3))
                run(evict_probs_t, u.back(2), 1)
                run(evict_pc, u.back(2), 0)
                run(sum_squares, u.back(3))
                run(exp, u.back(1), 0)
                run(take_log_2, u.back(3))
                run(evict_pc, u.back(2), 1)
                if in_step(u, 0):
                    evict_wqk()
                if in_step(u, 3):
                    take_log_1(3)
                run(take_rstd_2, u.back(3))
                run(evict_xt, u)
                if in_step(u, 0):
                    take_log_1(1)
                run(evict_probs_t, u.back(1), 0)
                run(exp, u.back(1), 1)
                run(scale_up_1, u.back(3))
                run(evict_tq, u)
                if in_step(u, 1):
                    take_log_1(2)
                run(evict_quant_t, u.back(4))

            act.preload_act_table_set("natural_log_exp_and_others")
            start_counts(act, "act")
            act.wait_ge(eps_ready, 1)
            pipeline(act, steps)

        @block.vector
        def _(dve):
            def take_moments_1(g):
                dve.wait_ge(x_in[g] if g < ALONE else x_ahead_in[g - ALONE], 16)
                for n in GROUPS[g]:
                    for h in range(2):
                        last = dve.bn_stats(stats_1[:, n, h], x_s[n][:, h] if g < ALONE else x_ahead[:, n - ALONE, h])
                last.then_inc(stats_ready, 1)
                dve.wait_ge(stats_ready, g + 1)
                for n in GROUPS[g]:
                    for h in range(2):
                        last = dve.bn_aggr(moments_1[:, n, h], stats_1[:, n, h])
                last.then_inc(moments_ready, 1)

            def row_max(p, h):
                slot = 2 * p.side + h
                dve.wait_ge(scores_made, count(p, 2, h))
                dve.tensor_reduce(neg_max[:, slot:slot + 1], ps_s[h][0:Q, 0:K], AX.X, ALU.max,
                                  negate=True).then_inc(max_ready, 1)

            def invert_sums(p):
                at = slice(2 * p.side, 2 * p.side + 2)
                dve.wait_ge(probs_ready, count(p, 2))
                dve.reciprocal(row_inv[:, at], row_sum[:, at]).then_inc(inv_ready, 1)

            def residual_1(p, h):
                slot = 2 * p.side + h
                dve.wait_ge(attn_made, count(p, 2, h))
                dve.wait_ge(inv_ready, count(p))
                dve.wait_ge(xb_ready, count(p))
                dve.wait_ge(xc_ready, count(p.back(2), 2))
                dve.wait_ge(x1b_ready, count(p.back(2)))
                dve.scalar_tensor_tensor(x1[p.side][:, h], ps_o[h][0:Q, DC:DC + DX], row_inv[:, slot:slot + 1],
                                         xb[p.side][:, h], ALU.mult, ALU.add,
                                         accum_out=sum_2[p.side][:, h:h + 1]).then_inc(x1_ready, 1)

            def take_abs_max(p):
                dve.wait_ge(xc_ready, count(p, 2))
                dve.tensor_reduce(abs_max[p.side][:], xc[p.side][:], AX.X, ALU.max,
                                  apply_absolute_value=True).then_inc(abs_max_ready, 1)

            def scale_max(p):
                dve.wait_ge(abs_max_ready, count(p))
                dve.wait_ge(rstd_2_ready, count(p))
                dve.tensor_tensor(h_max[p.side][:], abs_max[p.side][:], rstd_2[p.side][:],
                                  ALU.mult).then_inc(h_max_ready, 1)

            def floor_max(p):
                dve.wait_ge(h_max_ready, count(p))
                dve.tensor_scalar(h_floored[p.side][:], h_max[p.side][:], AMAX_FLOOR, None,
                                  ALU.max).then_inc(h_floored_ready, 1)

            def invert_max(p):
                dve.wait_ge(h_floored_ready, count(p))
                dve.reciprocal(h_inv[p.side][:], h_floored[p.side][:]).then_inc(h_inv_ready, 1)

            def take_q_scale(p):
                dve.wait_ge(h_inv_ready, count(p))
                dve.scalar_tensor_tensor(q_scale[p.side][:], h_inv[p.side][:], FP8_MAX, rstd_2[p.side][:],
                                         ALU.mult, ALU.mult).then_inc(q_scale_ready, 1)

            def scale_up_0(p):
                dve.wait_ge(q_scale_ready, count(p))
                dve.tensor_scalar(scaled[p.side][:, 0], xc[p.side][:, 0], q_scale[p.side][:, 0:1],
                                  None, ALU.mult).then_inc(scaled_0_ready, 1)

            def take_power(p):
                dve.wait_ge(scaled_0_ready, count(p))
                dve.wait_ge(scaled_1_ready, count(p))
                dve.tensor_scalar(power[p.side][:].bitcast(u16), scaled[p.side][:].bitcast(u16), 0x7F80, 0x0040,
                                  ALU.bitwise_and, ALU.bitwise_or).then_inc(power_ready, 1)

            def floor_power(p):
                dve.wait_ge(power_ready, count(p))
                dve.wait_ge(quant_ready, count(p.back(2)))
                dve.tensor_scalar(magic[p.side][:], power[p.side][:], 1.5 * 2.0 ** -6, 2.0 ** 20,
                                  ALU.max, ALU.mult).then_inc(magic_ready, 1)

            def shift(p):
                dve.wait_ge(magic_ready, count(p))
                for h in range(2):
                    dve.scalar_tensor_tensor(shifted[p.side][:, h], xc[p.side][:, h], q_scale[p.side][:, h:h + 1],
                                             magic[p.side][:, h], ALU.mult, ALU.add).then_inc(shifted_ready, 1)

            def unshift_second(p):
                dve.wait_ge(shifted_ready, count(p, 2))
                dve.wait_ge(quant_t_made, count(p.back(2)))
                dve.tensor_tensor(quant[p.side][:, 1], shifted[p.side][:, 1], magic[p.side][:, 1],
                                  ALU.subtract).then_inc(second_quant_ready, 1)

            def residual_2(p, h):
                dve.wait_ge(linear_made, count(p))
                dve.wait_ge(x1b_ready, count(p))
                dve.wait_ge(out_scale_ready, count(p))
                dve.wait_ge(stored[p.side], 16 * (p.turn + 1))
                dve.scalar_tensor_tensor(out_s[p.side][:, h], ps_f[0:Q, h * DX:(h + 1) * DX],
                                         out_scale[p.side][:, h:h + 1], x1b[p.side][:, h],
                                         ALU.mult, ALU.add).then_inc(out_ready, 1)

            def decode_weights():
                def after(i):
                    dve.wait_ge(w_step, i)

                dve.wait_ge(w8_in, 16)
                dve.tensor_copy(w_bits[:], w8[:]).then_inc(w_step, 1)
                after(1)
                dve.tensor_scalar(w_mag[:], w_bits[:], 0x7F, 20, ALU.bitwise_and, ALU.logical_shift_left).then_inc(w_step, 1)
                dve.tensor_scalar(w_sign[:], w_bits[:], 0x80, 24, ALU.bitwise_and, ALU.logical_shift_left).then_inc(w_step, 1)
                after(2)
                dve.tensor_scalar(w_sub[:], w_mag[:], 7.0 * 2 ** 20, 2.0 ** -29, ALU.min, ALU.mult).then_inc(w_step, 1)
                after(4)
                dve.scalar_tensor_tensor(w_abs[:], w_mag[:].bitcast(fp32), 2.0 ** 120, w_sub[:],
                                         ALU.mult, ALU.max).then_inc(w_step, 1)
                after(5)
                dve.tensor_tensor(w_bits[:], w_abs[:].bitcast(u32), w_sign[:], ALU.bitwise_or).then_inc(w_step, 1)
                after(6)
                dve.tensor_copy(w_b[:], w_bits[:].bitcast(fp32)).then_inc(w_step, 1)

            def scale_weight_scale():
                dve.wait_ge(ws_in, 16)
                dve.tensor_scalar(ws448[:], ws_s[:], 1.0 / FP8_MAX, None, ALU.mult).then_inc(ws_ready, 1)

            def steps(u):
                run(take_abs_max, u.back(3))
                run(residual_1, u.back(2), 0)
                run(scale_max, u.back(3))
                if in_step(u, 0):
                    take_moments_1(0)
                    take_moments_1(1)
                if in_step(u, 2):
                    scale_weight_scale()
                run(floor_max, u.back(3))
                if in_step(u, 0):
                    decode_weights()
                run(invert_max, u.back(3))
                run(take_q_scale, u.back(3))
                if in_step(u, 1):
                    take_moments_1(2)
                run(residual_1, u.back(2), 1)
                run(scale_up_0, u.back(3))
                if in_step(u, 2):
                    take_moments_1(3)
                run(invert_sums, u.back(1))
                run(take_power, u.back(3))
                run(floor_power, u.back(3))
                run(shift, u.back(3))
                if is_last(u.back(3)):
                    unshift_second(u.back(3))
                run(row_max, u, 0)
                run(row_max, u, 1)
                run(residual_2, u.back(4), 1)
                run(residual_2, u.back(4), 0)

            dve.memset(warm[:], 0.0).then_inc(warm_set, 1)
            start_counts(dve, "dve")
            for i in range(2):
                dve.sem_inc(stored[i], 16)
            dve.memset(eps_s[:], EPS).then_inc(eps_ready, 1)
            pipeline(dve, steps)

        @block.tensor
        def _(pe):
            def keep_warm(products):
                for _ in range(products):
                    pe.matmul(ps_f[:], warm[:, 0:128], warm[:], start=True, stop=True)

            def transpose_x(p):
                pe.wait_ge(xn_ready, count(p))
                pe.wait_ge(tq_ready, count(p.back(1)))
                for c in range(XC):
                    for h in range(2):
                        at = (2 * c + h) * Q
                        last = pe.transpose(ps_x[:, at:at + Q], xn[p.side][:, h, 128 * c:128 * (c + 1)], ident[0:Q, 0:Q])
                last.then_inc(xt_made, 1)

            def project(p):
                pe.wait_ge(wqk_ready, 2)
                pe.wait_ge(xt_ready, count(p))
                for c in range(XC):
                    last = pe.matmul(ps_x[:, 0:2 * Q], wqk[:, c], xn_t[p.side][:, c], start=c == 0, stop=c == XC - 1)
                last.then_inc(tq_made, 1)

            def score(p, h):
                pe.wait_ge(tq_ready, count(p))
                pe.wait_ge(ctx_t_in[p.side], 16 * (p.turn + 1))
                pe.wait_ge(probs_ready, count(p.back(1), 2, h))
                pe.matmul(ps_s[h][0:Q, 0:K], tq_t[p.side][:, h], ctx_ts[p.side][:, h], start=True, stop=True)\
                    .then_inc(scores_made, 1)

            def transpose_probs(p, h):
                pe.wait_ge(probs_ready, count(p, 2, h))
                pe.wait_ge(probs_t_ready, count(p, 2, h, before=1))
                for j in range(KJ):
                    last = pe.transpose(ps_p[0:KP, j * Q:(j + 1) * Q], probs[h][:, j * KP:(j + 1) * KP], ident[0:Q, 0:Q])
                last.then_inc(probs_t_made, 1)

            def attend(p, h):
                pe.wait_ge(probs_t_ready, count(p, 2, h))
                pe.wait_ge(ctx_in[p.side], 32 * (p.turn + 1))
                pe.wait_ge(x1_ready, count(p.back(1), 2, h))
                for j in range(KJ):
                    last = pe.matmul(ps_o[h][:, 0:Q], ctx_s[p.side][:, h, j], probs_t[h][:, j], start=j == 0, stop=j == KJ - 1)
                last.then_inc(pc_made, 1)

            def value(p, h):
                pe.wait_ge(wv_in, 16)
                pe.wait_ge(pc_ready, count(p, 2, h))
                pe.matmul(ps_o[h][0:Q, DC:DC + DX], pc_t[h][:], wv_s[:], start=True, stop=True).then_inc(attn_made, 1)

            def transpose_quant(p):
                pe.wait_ge(quant_ready, count(p))
                if is_last(p):
                    pe.wait_ge(second_quant_ready, 1)
                pe.wait_ge(quant_t_ready, count(p.back(1)))
                for c in range(XC):
                    for h in range(2):
                        at = (2 * c + h) * Q
                        last = pe.transpose(ps_q[:, at:at + Q], quant[p.side][:, h, 128 * c:128 * (c + 1)], ident_b[0:Q, 0:Q])
                last.then_inc(quant_t_made, 1)

            def linear(p):
                pe.wait_ge(w_step, 7)
                pe.wait_ge(quant_t_ready, count(p))
                pe.wait_ge(out_ready, count(p.back(1), 2))
                for h in range(2):
                    for c in range(XC):
                        last = pe.matmul(ps_f[0:Q, h * DX:(h + 1) * DX], quant_t[p.side][:, c, h], w_b[:, c],
                                         start=c == 0, stop=c == XC - 1)
                last.then_inc(linear_made, 1)

            def steps(u):
                run(value, u.back(2), 0)
                run(transpose_x, u)
                if in_step(u, 0):
                    keep_warm(4)
                run(transpose_probs, u.back(1), 0)
                run(transpose_quant, u.back(4))
                run(value, u.back(2), 1)
                run(project, u)
                if in_step(u, 0):
                    keep_warm(3)
                run(attend, u.back(1), 0)
                run(transpose_probs, u.back(1), 1)
                run(score, u, 0)
                run(score, u, 1)
                run(linear, u.back(4))
                run(attend, u.back(1), 1)

            start_counts(pe, "pe")
            pe.wait_ge(warm_set, 1)
            keep_warm(7)
            pe.wait_ge(wqk_in, 48)
            for i in range(XC):
                for e in range(XC):
                    last = pe.matmul(ps_s[0][:, i * DC:(i + 1) * DC], wq_ts[:, e, 128 * i:128 * (i + 1)], wk_ts[:, e],
                                     start=e == 0, stop=e == XC - 1)
            last.then_inc(wqk_made, 1)
            for e in range(XC):
                last = pe.matmul(ps_s[1][:, 0:1], wk_ts[:, e], bq_s[:, e:e + 1], start=e == 0, stop=e == XC - 1)
            last.then_inc(wqk_made, 1)
            pe.wait_ge(ident_ready, 2)
            pipeline(pe, steps)


def kernel(x, ctx_512, L0_xattn_Wq, L0_xattn_bq, L0_xattn_Wk, L0_xattn_bk, L0_xattn_Wv, L0_xattn_bv,
           L0_ffn_weight, L0_ffn_weight_scale, L0_ffn_bias):
    import numpy as np
    import concourse.bacc as bacc
    from concourse.bass_utils import run_bass_kernel_spmd

    ctx = np.asarray(ctx_512)
    arrays = {
        "x": np.asarray(x),
        "ctx": ctx,
        "ctx_t": ctx.reshape(B, KP, KJ, DC).transpose(0, 3, 2, 1).reshape(B, DC, K),
        "wq_t": np.asarray(L0_xattn_Wq).T,
        "wk_t": np.asarray(L0_xattn_Wk).T,
        "wv": np.asarray(L0_xattn_Wv),
        "bq": np.asarray(L0_xattn_bq).reshape(XC, 128).T,
        "bv": np.asarray(L0_xattn_bv),
        "w_t": np.asarray(L0_ffn_weight).T.view(np.uint8),
        "w_scale": np.asarray(L0_ffn_weight_scale).reshape(1, 1),
        "bias": np.asarray(L0_ffn_bias),
    }
    arrays = {f"in_{k}": np.ascontiguousarray(v) for k, v in arrays.items()}
    nc = bacc.Bacc("TRN2", target_bir_lowering=False, num_devices=1)
    args = [nc.dram_tensor(k, v.shape, mybir.dt.from_np(v.dtype), kind="ExternalInput").ap() for k, v in arrays.items()]
    args.append(nc.dram_tensor("out_0", (B, Q, DX), mybir.dt.float32, kind="ExternalOutput").ap())
    xattn_ffn_kernel(nc, *args)
    return run_bass_kernel_spmd(nc, [arrays], core_ids=[0]).results[0]["out_0"]
```
